# Optimizing a Trainium2 kernel written in Bass

```python
import numpy as np
import jax
import jax.numpy as jnp

def _softmax(x, axis=-1):
    return jax.nn.softmax(x, axis=axis)

def _gelu(x):
    return jax.nn.gelu(x, approximate=True)

def _silu(x):
    return jax.nn.silu(x)

def _sigmoid(x):
    return jax.nn.sigmoid(x)

def _layernorm(x, axis=-1, eps=1e-05):
    m = jnp.mean(x, axis=axis, keepdims=True)
    v = jnp.var(x, axis=axis, keepdims=True)
    return (x - m) / jnp.sqrt(v + eps)

def _scatter_add(tgt, idx, src, axis=0):
    return tgt.at[idx].add(src)

def _segment_sum(src, seg, n):
    return jax.ops.segment_sum(src, seg, n)
kernel_name = 'mk_xattn_seq_d1_seqx_r2_015b94'

def setup_inputs(seed: int=0):
    np.random.seed(seed)
    _w = jnp.asarray

    def _rec_inputs():
        import jax
        import jax.numpy as jnp
        _rk = jax.random.key(seed)
        x = -0.0001108 + 0.9999 * jax.random.normal(jax.random.fold_in(_rk, 1), (2, 2048, 640), jnp.float32)
        _lenS = 2048 - jax.random.randint(jax.random.fold_in(_rk, 7), (2,), 0, max(1, 2048 // 4) + 1, jnp.int32)
        _lenS2 = 77 - jax.random.randint(jax.random.fold_in(_rk, 8), (2,), 0, max(1, 77 // 4) + 1, jnp.int32)
        _ctx_2048P = jax.random.normal(jax.random.fold_in(_rk, 11), (2, 16, 1024), jnp.float32)
        _ctx_2048c = jax.random.dirichlet(jax.random.fold_in(_rk, 511), 0.3 * jnp.ones((16,), jnp.float32), (2, 77))
        _ctx_2048t = jnp.einsum('bsk,bkd->bsd', _ctx_2048c, _ctx_2048P)
        _ctx_2048t = _ctx_2048t * jax.lax.rsqrt(jnp.mean(jnp.square(_ctx_2048t)) + 1e-12) * 0.953939
        ctx_2048 = -0.000395056 + 1.00006 * (_ctx_2048t + 0.3 * jax.random.normal(jax.random.fold_in(_rk, 611), (2, 77, 1024), jnp.float32))
        return (x, ctx_2048)
    x, ctx_2048 = _rec_inputs()

    def _L0_xattn_setup():
        import jax, jax.numpy as jnp
        import numpy as np
        NUM_HEADS = 20
        TEXT_LEN = 77
        IP_SCALE = 1.0

        def _attend(q, k, v, sm_scale):
            scores = jnp.einsum('bhsd,bhld->bhsl', q, k) * sm_scale
            probs = jax.nn.softmax(scores, axis=-1)
            return jnp.einsum('bhsl,bhld->bhsd', probs, v)

        def _split_heads(x, h):
            b, s, c = x.shape
            return x.reshape(b, s, h, c // h).transpose(0, 2, 1, 3)

        def _merge_heads(x):
            b, h, s, d = x.shape
            return x.transpose(0, 2, 1, 3).reshape(b, s, h * d)
        key = jax.random.key(seed)
        ks = jax.random.split(key, 8)
        B, S, C, CC, L = (8, 2048, 640, 1024, TEXT_LEN + 4)
        sd_q = 1.0 / np.sqrt(C)
        sd_kv = 1.0 / np.sqrt(CC)
        return {'hidden_states': jax.random.normal(ks[0], (B, S, C), jnp.float32), 'encoder_hidden_states': jax.random.normal(ks[1], (B, L, CC), jnp.float32), 'Wq': jax.random.normal(ks[2], (C, C), jnp.float32) * sd_q, 'Wk': jax.random.normal(ks[3], (C, CC), jnp.float32) * sd_kv, 'Wv': jax.random.normal(ks[4], (C, CC), jnp.float32) * sd_kv, 'Wk_ip': jax.random.normal(ks[5], (C, CC), jnp.float32) * sd_kv, 'Wv_ip': jax.random.normal(ks[6], (C, CC), jnp.float32) * sd_kv, 'Wo': jax.random.normal(ks[7], (C, C), jnp.float32) * sd_q, 'bo': jnp.zeros((C,), jnp.float32)}
    _L0_xattn_all = _L0_xattn_setup()
    _L0_xattn_in = {k: v for k, v in _L0_xattn_all.items() if k in ('Wq', 'Wk', 'Wv', 'Wk_ip', 'Wv_ip', 'Wo', 'bo')}
    del _L0_xattn_all
    return {'x': x, 'ctx_2048': ctx_2048, 'L0_xattn_Wq': _L0_xattn_in['Wq'], 'L0_xattn_Wk': _L0_xattn_in['Wk'], 'L0_xattn_Wv': _L0_xattn_in['Wv'], 'L0_xattn_Wk_ip': _L0_xattn_in['Wk_ip'], 'L0_xattn_Wv_ip': _L0_xattn_in['Wv_ip'], 'L0_xattn_Wo': _L0_xattn_in['Wo'], 'L0_xattn_bo': _L0_xattn_in['bo']}

def reference(x, ctx_2048, L0_xattn_Wq, L0_xattn_Wk, L0_xattn_Wv, L0_xattn_Wk_ip, L0_xattn_Wv_ip, L0_xattn_Wo, L0_xattn_bo):
    import jax
    import jax.numpy as jnp

    def _L0_xattn_ref(hidden_states, encoder_hidden_states, Wq, Wk, Wv, Wk_ip, Wv_ip, Wo, bo):
        import jax, jax.numpy as jnp
        import numpy as np
        NUM_HEADS = 20
        TEXT_LEN = 77
        IP_SCALE = 1.0

        def _attend(q, k, v, sm_scale):
            scores = jnp.einsum('bhsd,bhld->bhsl', q, k) * sm_scale
            probs = jax.nn.softmax(scores, axis=-1)
            return jnp.einsum('bhsl,bhld->bhsd', probs, v)

        def _split_heads(x, h):
            b, s, c = x.shape
            return x.reshape(b, s, h, c // h).transpose(0, 2, 1, 3)

        def _merge_heads(x):
            b, h, s, d = x.shape
            return x.transpose(0, 2, 1, 3).reshape(b, s, h * d)
        residual = hidden_states
        B, S, C = hidden_states.shape
        H = NUM_HEADS
        D = C // H
        sm_scale = 1.0 / jnp.sqrt(jnp.asarray(D, hidden_states.dtype))
        text = encoder_hidden_states[:, :TEXT_LEN, :]
        ip = encoder_hidden_states[:, TEXT_LEN:, :]
        q = _split_heads(hidden_states @ Wq.T, H)
        k = _split_heads(text @ Wk.T, H)
        v = _split_heads(text @ Wv.T, H)
        out_text = _merge_heads(_attend(q, k, v, sm_scale))
        k_ip = _split_heads(ip @ Wk_ip.T, H)
        v_ip = _split_heads(ip @ Wv_ip.T, H)
        out_ip = _merge_heads(_attend(q, k_ip, v_ip, sm_scale))
        out = out_text + IP_SCALE * out_ip
        out = out @ Wo.T + bo
        return out + residual
    x = _L0_xattn_ref(x, ctx_2048, L0_xattn_Wq, L0_xattn_Wk, L0_xattn_Wv, L0_xattn_Wk_ip, L0_xattn_Wv_ip, L0_xattn_Wo, L0_xattn_bo)
    return x

_drawn_inputs = setup_inputs


def setup_inputs(seed=0):
    import zlib

    import numpy as np

    out = dict(_drawn_inputs(seed))
    spreads = {'L0_xattn_bo': (0.0, 0.1)}
    factors = {}
    for name, (base, spread) in spreads.items():
        noise = np.random.default_rng([zlib.crc32(name.encode()), seed]).standard_normal(out[name].shape)
        drawn = base * np.exp(spread * noise) if base else spread * noise
        out[name] = jnp.asarray(drawn.astype(out[name].dtype))
    for name, factor in factors.items():
        out[name] = (out[name] * factor).astype(out[name].dtype)
    return out
```

```python
import numpy as np
from contextlib import ExitStack

import concourse.bass as bass
from concourse import mybir

F32 = mybir.dt.float32
F32R = mybir.dt.float32r
F16 = mybir.dt.float16
ALU = mybir.AluOpType
ACT = mybir.ActivationFunctionType
AX_X = mybir.AxisListType.X

HEADS = 20
P = 128
TB = 512
MM32 = 3


def xattn_kernel(nc, x, ctx, wq, wk, wv, wo, bo, out):
    NB, _, G, _ = x.shape
    C = G * P
    HG = HEADS // G
    D = C // HEADS
    CC = ctx.shape[1]
    BL = ctx.shape[2]
    B = 2
    L = BL // B
    BPB = NB // B
    NU = NB * G
    TT = TB // P
    SCALE = float(D) ** -0.5
    TINY = 1e-30
    RS = 3
    KR = 3 * D + 1

    def split(u):
        return u // G, u % G

    def slot_uses(u):
        t, g = split(u)
        per_block = len([h for h in range(G) if h % RS == g % RS])
        return per_block * t + g // RS + 1

    def slot_before(u):
        g = u % G
        return next(v for v in range(u - 1, u - 2 * G, -1) if v % G % RS == g % RS)

    def out_tiles(s):
        t, g = split(s)
        if not 1 <= t <= NB:
            return []
        return [(t - 1, k) for k in {1: (0, 1), 2: (2, 3), 3: (4,)}.get(g, ())]

    def attn_splits(s):
        t, g = split(s)
        if g == 4 and 0 <= t < NB:
            return [(t, c) for c in (0, 1, 2)]
        if g == 0 and 1 <= t <= NB:
            return [(t - 1, c) for c in (3, 4)]
        return []

    STEPS = range(-2, NU + 5)

    with ExitStack() as stack:
        def sb(name, shape, dt, into=stack):
            return into.enter_context(nc.sbuf_tensor(name, shape, dt))

        def sem(name):
            return stack.enter_context(nc.semaphore(name))

        wq_hi = sb("wq_hi", [P, G, C], F32R)
        wq_lo = sb("wq_lo", [P, G, C], F32R)
        wo_hi = sb("wo_hi", [P, G, C], F32R)
        wo_lo = sb("wo_lo", [P, G, C], F32R)
        k_packed = sb("k_packed", [P, G, HG, BL], F32R)
        k_diag = sb("k_diag", [P, G, B, HG * L], F32R)
        v_hi = sb("v_hi", [L, B, C], F16)
        v_lo = sb("v_lo", [L, B, C], F16)
        v_scale = sb("v_scale", [P, G], F32)
        v_inv = sb("v_inv", [P, G], F32)
        bias = sb("bias", [P, G], F32)
        ident = sb("ident", [P, P], F32)
        ones = sb("ones", [L, D], F16)
        x_f = sb("x_f", [P, G, TB], F32)
        x_hi = sb("x_hi", [P, G, TB], F32R)
        x_lo = sb("x_lo", [P, G, TB], F32R)
        q_hi = sb("q_hi", [P, RS, TB], F32R)
        q_lo = sb("q_lo", [P, RS, TB], F32R)
        q_packed = sb("q_packed", [P, RS, HG, TB], F32R)
        mx = sb("mx", [P, RS, HG, TT], F32)
        mxT = sb("mxT", [HG * TT, RS, P], F32R)

        early = ExitStack()
        stage_a = sb("stage_a", [P, CC, C], F32, early)
        stage_b = sb("stage_b", [P, CC, C], F32, early)
        ctx_sb = sb("ctx_sb", [P, CC, BL], F32, early)
        vT = sb("vT", [P, G, BL], F32, early)
        k_hi = sb("k_hi", [P, G, BL], F32R, early)
        k_lo = sb("k_lo", [P, G, BL], F32R, early)
        early.close()
        p_f = sb("p_f", [L, 2, TB], F32)
        p_hi = sb("p_hi", [L, HG, TB], F16)
        p_lo = sb("p_lo", [L, HG, TB], F16)
        rden = sb("rden", [P, TB], F32)
        attn = sb("attn", [P, G, TB], F32)
        attn_hi = sb("attn_hi", [P, G, TB], F32R)
        attn_lo = sb("attn_lo", [P, G, TB], F32R)
        x_res = sb("x_res", [P, RS, TB], F32)
        out_sb = sb("out_sb", [P, RS, TB], F32)

        def bank(name):
            return stack.enter_context(nc.psum_tensor(name, [P, 512], F32))

        ps_q, ps_o, ps_pv, ps_den = bank("ps_q"), bank("ps_o"), bank("ps_pv"), bank("ps_den")
        ps_s = [bank("ps_s0"), bank("ps_s1")]
        ps_m = [bank("ps_m0"), bank("ps_m1")]
        ps_mT = ps_m[0][0:HG * TT, 512 - P:512]

        wq_in, wk_in, wv_in, wo_in, ctx_in, bias_in = (sem(n) for n in (
            "wq_in", "wk_in", "wv_in", "wo_in", "ctx_in", "bias_in"))
        wq_hi_done, wq_lo_done, wo_hi_done, wo_lo_done = (sem(n) for n in (
            "wq_hi_done", "wq_lo_done", "wo_hi_done", "wo_lo_done"))
        zero_done, const_done, diag_done, kpack_in = (sem(n) for n in ("zero_done", "const_done", "diag_done", "kpack_in"))
        kproj_done, khi_done, klo_done = (sem(n) for n in ("kproj_done", "khi_done", "klo_done"))
        vproj_done, vmax_done, vinv_done, vT_done, vtr_done, vhi_done, vlo_done = (sem(n) for n in (
            "vproj_done", "vmax_done", "vinv_done", "vT_done", "vtr_done", "vhi_done", "vlo_done"))
        x_in, xhi_done, xlo_done = sem("x_in"), sem("xhi_done"), sem("xlo_done")
        q_done, qhi_done, qlo_done = sem("q_done"), sem("qhi_done"), sem("qlo_done")
        pack_in = [sem(f"pack_in{i}") for i in range(RS)]
        PACK = 16 * (3 * HG + 1)
        ms_done, max_done, mT_done, mT_copied = sem("ms_done"), sem("max_done"), sem("mT_done"), sem("mT_copied")
        s_done, pf_done, phi_done = sem("s_done"), sem("pf_done"), sem("phi_done")
        plo_dve, plo_pool = sem("plo_dve"), sem("plo_pool")
        pv_done, rden_done, norm_done = sem("pv_done"), sem("rden_done"), sem("norm_done")
        ahi_done, alo_done = sem("ahi_done"), sem("alo_done")
        o_done, outs_done = sem("o_done"), sem("outs_done")
        res_in = [sem(f"res_in{i}") for i in range(RS)]
        out_in = [sem(f"out_in{i}") for i in range(RS)]

        block = stack.enter_context(nc.Block())

        @block.sync
        def _(sp):
            sp.dma_start(stage_a[:, 0:G, :], wq).then_inc(wq_in, 16)
            sp.dma_start(x_f[:, :, :], x[0]).then_inc(x_in, 16)
            sp.dma_start(ctx_sb[:, :, :], ctx).then_inc(ctx_in, 16)
            sp.dma_start(stage_b[:, :, :], wk).then_inc(wk_in, 16)
            sp.dma_start(bias[:, :], bo).then_inc(bias_in, 16)
            sp.wait_ge(wq_hi_done, G)
            sp.wait_ge(wq_lo_done, G)
            sp.dma_start(stage_a[:, :, :], wv).then_inc(wv_in, 16)
            sp.wait_ge(kproj_done, G)
            sp.dma_start(stage_b[:, 0:G, :], wo).then_inc(wo_in, 16)
            sp.wait_ge(khi_done, G)
            sp.wait_ge(klo_done, G)
            for i in range(HG):
                for row, src in ((0, k_hi), (D, k_hi), (2 * D, k_lo)):
                    sp.dma_start(k_packed[row:row + D, :, i, :].bitcast(F32),
                                 src[D * i:D * (i + 1), :, :].bitcast(F32)).then_inc(kpack_in, 16)

            def load_x(t):
                sp.wait_ge(xhi_done, G * t)
                sp.wait_ge(xlo_done, G * t)
                sp.dma_start(x_f[:, :, :], x[t]).then_inc(x_in, 16)

            def load_max(u):
                t, g = split(u)
                sp.wait_ge(mT_copied, u + 1)
                if slot_before(u) >= 0:
                    sp.wait_ge(s_done, HG * (slot_before(u) + 1))
                sp.dma_start(q_packed[3 * D:KR, g % RS, :, :].bitcast(F32).rearrange("o i (a c) -> o (i a) c", c=P),
                             mxT[:, g % RS, :].bitcast(F32)).then_inc(pack_in[g % RS], 16)

            def pack_q(u):
                t, g = split(u)
                if slot_before(u) >= 0:
                    sp.wait_ge(s_done, HG * (slot_before(u) + 1))
                sp.wait_ge(qhi_done, u + 1)
                for row, src, done in ((0, q_hi, None), (2 * D, q_hi, None), (D, q_lo, qlo_done)):
                    if done is not None:
                        sp.wait_ge(done, u + 1)
                    for i in range(HG):
                        sp.dma_start(q_packed[row:row + D, g % RS, i, :].bitcast(F32),
                                     src[D * i:D * (i + 1), g % RS, :].bitcast(F32)).then_inc(pack_in[g % RS], 16)

            for s in STEPS:
                if 0 <= s + 1 < NU:
                    load_max(s + 1)
                if 0 <= s + 2 < NU:
                    pack_q(s + 2)
                if s % G == 3 and 0 <= s // G + 2 < NB:
                    load_x(s // G + 2)

        @block.gpsimd
        def _(pool):
            nc.gpsimd.memset(k_diag[:, :, :, :].bitcast(F32), 0.0).then_inc(const_done, 1)
            pool.wait_ge(const_done, 1)
            nc.gpsimd.memset(k_packed[3 * D:KR, :, :, :].bitcast(F32), -1.0).then_inc(const_done, 1)
            pool.wait_ge(const_done, 2)
            nc.gpsimd.memset(ones[:, :], 1.0).then_inc(const_done, 1)
            pool.wait_ge(const_done, 3)
            nc.gpsimd.memset(ident[:, :], 0.0).then_inc(zero_done, 1)
            pool.wait_ge(zero_done, 1)
            nc.gpsimd.affine_select(out=ident[:, :], in_=ident[:, :], compare_op=ALU.not_equal, fill=1.0,
                                    base=0, pattern=[[-1, P]], channel_multiplier=1).then_inc(const_done, 1)

            def x_low(t):
                for c in range(G):
                    pool.wait_ge(xhi_done, G * t + c + 1)
                    nc.gpsimd.tensor_tensor(x_lo[:, c, :], x_f[:, c, :], x_hi[:, c, :].bitcast(F32),
                                            ALU.subtract).then_inc(xlo_done, 1)

            x_low(0)
            pool.wait_ge(wo_in, 16)
            for c in range(G):
                pool.wait_ge(wo_hi_done, c + 1)
                nc.gpsimd.tensor_tensor(wo_lo[:, c, :], stage_b[:, c, :], wo_hi[:, c, :].bitcast(F32),
                                        ALU.subtract).then_inc(wo_lo_done, 1)

            for s in STEPS:
                if 0 <= s < NU:
                    for i in (1, 3):
                        pool.wait_ge(phi_done, HG * s + i + 1)
                        pool.wait_ge(pf_done, HG * s + i + 1)
                        if s >= 1:
                            pool.wait_ge(pv_done, s)
                        nc.gpsimd.tensor_tensor(p_lo[:, i, :], p_f[:, i % 2, :], p_hi[:, i, :],
                                                ALU.subtract).then_inc(plo_pool, 1)
                for t, c in attn_splits(s):
                    pool.wait_ge(ahi_done, G * t + c + 1)
                    nc.gpsimd.tensor_tensor(attn_lo[:, c, :], attn[:, c, :], attn_hi[:, c, :].bitcast(F32),
                                            ALU.subtract).then_inc(alo_done, 1)
                if s % G == 3 and 0 <= s // G + 1 < NB:
                    if s < 0:
                        continue
                    x_low(s // G + 1)

        @block.scalar
        def _(act):
            def x_high(t):
                act.wait_ge(x_in, 16 * (t + 1))
                if t >= 1:
                    act.wait_ge(q_done, G * t)
                for c in range(G):
                    nc.scalar.copy(x_hi[:, c, :], x_f[:, c, :]).then_inc(xhi_done, 1)

            act.wait_ge(wq_in, 16)
            for c in range(G):
                nc.scalar.copy(wq_hi[:, c, :], stage_a[:, c, :]).then_inc(wq_hi_done, 1)
            x_high(0)

            def q_high(u):
                t, g = split(u)
                act.wait_ge(q_done, u + 1)
                if slot_before(u) >= 0:
                    act.wait_ge(s_done, HG * (slot_before(u) + 1))
                nc.scalar.copy(q_hi[:, g % RS, :], ps_q[:, :]).then_inc(qhi_done, 1)

            def start_k():
                for g in range(G):
                    act.wait_ge(kproj_done, g + 1)
                    nc.scalar.copy(k_hi[:, g, :], ps_s[g % 2][:, 0:BL]).then_inc(khi_done, 1)
                act.wait_ge(const_done, 1)
                act.wait_ge(khi_done, G)
                for i in range(HG):
                    for b in range(B):
                        rows = slice(D * i, D * (i + 1))
                        nc.scalar.copy(k_diag[rows, :, b, L * i:L * (i + 1)],
                                       k_hi[rows, :, L * b:L * (b + 1)].bitcast(F32)).then_inc(diag_done, 1)

            def start_v():
                for n in range(G * B):
                    act.wait_ge(vtr_done, n + 1)
                    g, b = n // B, n % B
                    nc.scalar.copy(v_hi[:, b, P * g:P * (g + 1)], ps_s[n % 2][0:L, 0:P]).then_inc(vhi_done, 1)
                act.wait_ge(wo_in, 16)
                for c in range(G):
                    nc.scalar.copy(wo_hi[:, c, :], stage_b[:, c, :]).then_inc(wo_hi_done, 1)

            for s in STEPS:
                if s == 0:
                    start_v()
                    act.wait_ge(wo_lo_done, G)
                    act.wait_ge(vlo_done, G * B)
                    act.wait_ge(kpack_in, 16 * 3 * HG)
                for t, c in attn_splits(s):
                    act.wait_ge(norm_done, G * t + c + 1)
                    if t >= 1:
                        act.wait_ge(o_done, G * t)
                    nc.scalar.copy(attn_hi[:, c, :], attn[:, c, :]).then_inc(ahi_done, 1)
                if 0 <= s < NU:
                    for i in range(HG):
                        n = HG * s + i
                        act.wait_ge(s_done, n + 1)
                        if i >= 2 or s >= 1:
                            if i % 2 == 0:
                                act.wait_ge(plo_dve, n // 2)
                            else:
                                act.wait_ge(plo_pool, n // 2)
                        nc.scalar.activation(p_f[:, i % 2, :], ps_s[i % 2][0:L, :], ACT.Exp,
                                             scale=SCALE).then_inc(pf_done, 1)
                        if s >= 1:
                            act.wait_ge(pv_done, s)
                        nc.scalar.activation(p_hi[:, i, :], ps_s[i % 2][0:L, :], ACT.Exp,
                                             scale=SCALE).then_inc(phi_done, 1)
                for t, k in out_tiles(s - 1):
                    act.wait_ge(outs_done, G * t + k + 1)
                    act.dma_start(out[t, k], out_sb[:, k % RS, :]).then_inc(out_in[k % RS], 16)
                if 0 <= s + 1 < NU:
                    g = (s + 1) % G
                    act.wait_ge(mT_done, s + 2)
                    if slot_before(s + 1) >= 0:
                        act.wait_ge(s_done, HG * (slot_before(s + 1) + 1))
                    nc.scalar.copy(mxT[:, g % RS, :], ps_mT).then_inc(mT_copied, 1)
                if s % G == 3 and 0 <= s and s // G + 1 < NB:
                    x_high(s // G + 1)
                if 0 <= s + 2 < NU:
                    q_high(s + 2)
                if s == -2:
                    start_k()
                for t, k in out_tiles(s + 1):
                    n = G * t + k
                    if slot_before(n) >= 0:
                        act.wait_ge(outs_done, slot_before(n) + 1)
                    else:
                        act.wait_ge(phi_done, 1)
                    act.dma_start(x_res[:, k % RS, :], x[t, :, k, :]).then_inc(res_in[k % RS], 16)
            for i in range(RS):
                act.wait_ge(out_in[i], 16 * NB * len([k for k in range(G) if k % RS == i]))

        @block.vector
        def _(dve):
            dve.wait_ge(wq_in, 16)
            for c in range(G):
                dve.wait_ge(wq_hi_done, c + 1)
                nc.vector.tensor_tensor(wq_lo[:, c, :], stage_a[:, c, :], wq_hi[:, c, :].bitcast(F32),
                                        ALU.subtract).then_inc(wq_lo_done, 1)

            def q_low(u):
                t, g = split(u)
                dve.wait_ge(qhi_done, u + 1)
                nc.vector.tensor_tensor(q_lo[:, g % RS, :], ps_q[:, :], q_hi[:, g % RS, :].bitcast(F32),
                                        ALU.subtract).then_inc(qlo_done, 1)

            def start_k():
                for g in range(G):
                    dve.wait_ge(khi_done, g + 1)
                    nc.vector.tensor_tensor(k_lo[:, g, :], ps_s[g % 2][:, 0:BL], k_hi[:, g, :].bitcast(F32),
                                            ALU.subtract).then_inc(klo_done, 1)

            def start_v():
                for g in range(G):
                    dve.wait_ge(vproj_done, g + 1)
                    nc.vector.tensor_reduce(v_scale[:, g:g + 1], ps_s[g % 2][:, 0:BL], AX_X, ALU.max,
                                            apply_absolute_value=True).then_inc(vmax_done, 1)
                    dve.wait_ge(vmax_done, 3 * g + 1)
                    nc.vector.tensor_scalar(v_scale[:, g:g + 1], v_scale[:, g:g + 1], TINY, None,
                                            ALU.max).then_inc(vmax_done, 1)
                    dve.wait_ge(vmax_done, 3 * g + 2)
                    nc.vector.reciprocal(v_inv[:, g:g + 1], v_scale[:, g:g + 1]).then_inc(vmax_done, 1)
                    dve.wait_ge(vmax_done, 3 * g + 3)
                    nc.vector.tensor_scalar(vT[:, g, :], ps_s[g % 2][:, 0:BL], v_inv[:, g:g + 1], None,
                                            ALU.mult).then_inc(vT_done, 1)
                for n in range(G * B):
                    g, b = n // B, n % B
                    dve.wait_ge(vhi_done, n + 1)
                    nc.vector.tensor_tensor(v_lo[:, b, P * g:P * (g + 1)], ps_s[n % 2][0:L, 0:P],
                                            v_hi[:, b, P * g:P * (g + 1)], ALU.subtract).then_inc(vlo_done, 1)
                dve.wait_ge(bias_in, 16)

            for s in STEPS:
                if s == 0:
                    start_v()
                if 0 <= s - 1 < NU:
                    t, g = split(s - 1)
                    dve.wait_ge(pv_done, s)
                    nc.vector.reciprocal(rden[:, :], ps_den[:, :]).then_inc(rden_done, 1)
                    dve.wait_ge(rden_done, s)
                    if t >= 1:
                        dve.wait_ge(ahi_done, G * (t - 1) + g + 1)
                        dve.wait_ge(alo_done, G * (t - 1) + g + 1)
                    nc.vector.scalar_tensor_tensor(attn[:, g, :], ps_pv[:, :], v_scale[:, g:g + 1], rden[:, :],
                                                   ALU.mult, ALU.mult).then_inc(norm_done, 1)
                if 0 <= s < NU:
                    for i in (0, 2):
                        dve.wait_ge(phi_done, HG * s + i + 1)
                        dve.wait_ge(pf_done, HG * s + i + 1)
                        nc.vector.tensor_tensor(p_lo[:, i, :], p_f[:, i % 2, :], p_hi[:, i, :],
                                                ALU.subtract).then_inc(plo_dve, 1)
                if 0 <= s + 1 < NU:
                    g = (s + 1) % G
                    for tt in range(TT):
                        dve.wait_ge(ms_done, TT * (s + 1) + tt + 1)
                        if slot_before(s + 1) >= 0:
                            dve.wait_ge(mT_done, slot_before(s + 1) + 1)
                        nc.vector.tensor_reduce(mx[:, g % RS, :, tt],
                                                ps_m[tt % 2][:, 0:HG * L].rearrange("p (h k) -> p h k", k=L),
                                                AX_X, ALU.max).then_inc(max_done, 1)
                for t, k in out_tiles(s):
                    n = G * t + k
                    dve.wait_ge(o_done, n + 1)
                    dve.wait_ge(res_in[k % RS], 16 * slot_uses(n))
                    if slot_before(n) >= 0:
                        dve.wait_ge(out_in[k % RS], 16 * (slot_uses(n) - 1))
                    nc.vector.scalar_tensor_tensor(out_sb[:, k % RS, :], ps_o[:, :], bias[:, k:k + 1],
                                                   x_res[:, k % RS, :], ALU.add, ALU.add).then_inc(outs_done, 1)
                if 0 <= s + 2 < NU:
                    q_low(s + 2)
                if s == -2:
                    start_k()

        @block.tensor
        def _(pe):
            def project(ps, w_hi, w_lo, a_hi, a_lo, k, ready=None):
                for c in range(G):
                    if ready is not None:
                        ready(c)
                    for n, (w, a) in enumerate(((w_hi, a_hi), (w_lo, a_hi), (w_hi, a_lo))):
                        last = nc.tensor.matmul(ps[:, :], w[:, c, P * k:P * (k + 1)], a[:, c, :],
                                                start=(c == 0 and n == 0), stop=(c == G - 1 and n == MM32 - 1))
                return last

            def project_q(u):
                t, g = split(u)

                def ready(c):
                    if u == 0:
                        pe.wait_ge(wq_hi_done, c + 1)
                        pe.wait_ge(wq_lo_done, c + 1)
                    if g == 0:
                        pe.wait_ge(xhi_done, G * t + c + 1)
                        pe.wait_ge(xlo_done, G * t + c + 1)
                if u >= 1:
                    pe.wait_ge(qlo_done, u)
                project(ps_q, wq_hi, wq_lo, x_hi, x_lo, g, ready).then_inc(q_done, 1)

            def project_ctx(w, ps, g):
                for c in range(CC):
                    last = nc.tensor.matmul(ps[:, 0:BL], w[:, c, P * g:P * (g + 1)], ctx_sb[:, c, :],
                                            start=(c == 0), stop=(c == CC - 1))
                return last

            def start_k():
                pe.wait_ge(wk_in, 16)
                pe.wait_ge(ctx_in, 16)
                for g in range(G):
                    if g >= 2:
                        pe.wait_ge(klo_done, g - 1)
                    project_ctx(stage_b, ps_s[g % 2], g).then_inc(kproj_done, 1)

            def start_v():
                pe.wait_ge(wv_in, 16)
                for g in range(G):
                    if g < 2:
                        pe.wait_ge(klo_done, G)
                    else:
                        pe.wait_ge(vT_done, g - 1)
                    project_ctx(stage_a, ps_s[g % 2], g).then_inc(vproj_done, 1)
                pe.wait_ge(const_done, 4)
                pe.wait_ge(vT_done, G)
                for n in range(G * B):
                    g, b = n // B, n % B
                    if n >= 2:
                        pe.wait_ge(vlo_done, n - 1)
                    nc.tensor.transpose(ps_s[n % 2][0:L, 0:P], vT[:, g, L * b:L * (b + 1)],
                                        ident[:, :]).then_inc(vtr_done, 1)

            def max_scores(u, tt):
                t, g = split(u)
                pe.wait_ge(qhi_done, u + 1)
                if tt >= 2:
                    pe.wait_ge(max_done, TT * u + tt - 1)
                elif u >= 1:
                    pe.wait_ge(max_done, TT * (u - 1) + tt + 3)
                    pe.wait_ge(mT_copied, u)
                nc.tensor.matmul(ps_m[tt % 2][:, 0:HG * L], q_hi[:, g % RS, P * tt:P * (tt + 1)],
                                 k_diag[:, g, t // BPB, :], start=True, stop=True).then_inc(ms_done, 1)

            def transpose_max(u):
                pe.wait_ge(max_done, TT * (u + 1))
                nc.tensor.transpose(ps_mT, mx[:, u % G % RS, :, :].rearrange("p i t -> p (i t)"),
                                    ident[:, :]).then_inc(mT_done, 1)

            def scores(u):
                t, g = split(u)
                b = t // BPB
                pe.wait_ge(pack_in[g % RS], PACK * slot_uses(u))
                for i in range(HG):
                    if i >= 2:
                        pe.wait_ge(phi_done, HG * u + i - 1)
                    elif u >= 1:
                        pe.wait_ge(phi_done, HG * (u - 1) + i + 3)
                    nc.tensor.matmul(ps_s[i % 2][0:L, :], k_packed[0:KR, g, i, L * b:L * (b + 1)],
                                     q_packed[0:KR, g % RS, i, :], start=True, stop=True).then_inc(s_done, 1)

            def values(u):
                t, g = split(u)
                b = t // BPB
                pe.wait_ge(phi_done, HG * (u + 1))
                pe.wait_ge(plo_dve, HG // 2 * (u + 1))
                pe.wait_ge(plo_pool, HG // 2 * (u + 1))
                if u >= 1:
                    pe.wait_ge(norm_done, u)
                for n, (v, p) in enumerate(((v_hi, p_hi), (v_lo, p_hi), (v_hi, p_lo))):
                    for i in range(HG):
                        nc.tensor.matmul(ps_pv[D * i:D * (i + 1), :], v[:, b, P * g + D * i:P * g + D * (i + 1)],
                                         p[:, i, :], start=(n == 0), stop=(n == 2), tile_position=(0, D * i))
                for n, p in enumerate((p_hi, p_lo)):
                    for i in range(HG):
                        last = nc.tensor.matmul(ps_den[D * i:D * (i + 1), :], ones[:, :], p[:, i, :],
                                                start=(n == 0), stop=(n == 1), tile_position=(0, D * i))
                last.then_inc(pv_done, 1)

            def project_out(t, k):
                n = G * t + k
                if k == 0:
                    pe.wait_ge(ahi_done, G * (t + 1))
                    pe.wait_ge(alo_done, G * (t + 1))
                if n >= 1:
                    pe.wait_ge(outs_done, n)
                project(ps_o, wo_hi, wo_lo, attn_hi, attn_lo, k).then_inc(o_done, 1)

            for s in STEPS:
                if s == 0:
                    start_v()
                    pe.wait_ge(vlo_done, G * B)
                if s == 1:
                    pe.wait_ge(wo_lo_done, G)
                if 0 <= s - 1 < NU:
                    values(s - 1)
                if s == 0:
                    pe.wait_ge(kpack_in, 16 * 3 * HG)
                if 0 <= s < NU:
                    scores(s)
                if s == -1:
                    pe.wait_ge(diag_done, HG * B)
                tiles = out_tiles(s)
                if 0 <= s + 1 < NU:
                    max_scores(s + 1, 0)
                    max_scores(s + 1, 1)
                if tiles:
                    project_out(*tiles[0])
                if 0 <= s + 1 < NU:
                    max_scores(s + 1, 2)
                    max_scores(s + 1, 3)
                if 0 <= s + 2 < NU and not tiles[1:]:
                    if not tiles:
                        if 0 <= s + 1 < NU:
                            transpose_max(s + 1)
                        project_q(s + 2)
                    else:
                        transpose_max(s + 1)
                        project_q(s + 2)
                else:
                    if tiles[1:]:
                        project_out(*tiles[1])
                    if 0 <= s + 1 < NU:
                        transpose_max(s + 1)
                    if 0 <= s + 2 < NU:
                        project_q(s + 2)
                if s == -2:
                    start_k()


def kernel(x, ctx_2048, L0_xattn_Wq, L0_xattn_Wk, L0_xattn_Wv, L0_xattn_Wk_ip, L0_xattn_Wv_ip, L0_xattn_Wo,
           L0_xattn_bo):
    import concourse.bacc as bacc
    from concourse.bass_utils import run_bass_kernel_spmd

    Bn, S, C = x.shape
    _, L, CC = ctx_2048.shape
    G = C // P
    NB = Bn * S // TB

    def w_layout(w):
        w = np.asarray(w)
        return np.ascontiguousarray(w.reshape(w.shape[0], -1, P).transpose(2, 1, 0))

    arrays = {
        "x": np.ascontiguousarray(np.asarray(x).reshape(NB, TB, G, P).transpose(0, 3, 2, 1)),
        "ctx": w_layout(np.asarray(ctx_2048).reshape(Bn * L, CC)),
        "wq": w_layout(L0_xattn_Wq),
        "wk": w_layout(L0_xattn_Wk),
        "wv": w_layout(L0_xattn_Wv),
        "wo": w_layout(L0_xattn_Wo),
        "bo": np.ascontiguousarray(np.asarray(L0_xattn_bo).reshape(G, P).T),
    }
    nc = bacc.Bacc("TRN2", target_bir_lowering=False, num_devices=1)
    aps = [nc.dram_tensor(f"in_{n}", a.shape, mybir.dt.from_np(a.dtype), kind="ExternalInput").ap()
           for n, a in arrays.items()]
    out = nc.dram_tensor("out", (NB, G, P, TB), F32, kind="ExternalOutput").ap()
    xattn_kernel(nc, *aps, out)
    r = run_bass_kernel_spmd(nc, [{f"in_{n}": a for n, a in arrays.items()}], core_ids=[0])
    got = r.results[0]["out"]
    return got.transpose(0, 3, 1, 2).reshape(Bn, S, C)
```

```python
import numpy as np
from contextlib import ExitStack

import concourse.bass as bass
from concourse import mybir

F32 = mybir.dt.float32
F32R = mybir.dt.float32r
F16 = mybir.dt.float16
ALU = mybir.AluOpType
ACT = mybir.ActivationFunctionType
AX_X = mybir.AxisListType.X

HEADS = 20
P = 128
TB = 512
MM32 = 3


def xattn_kernel(nc, x, ctx, wq, wk, wv, wo, bo, out):
    NB, _, G, _ = x.shape
    C = G * P
    HG = HEADS // G
    D = C // HEADS
    CC = ctx.shape[1]
    BL = ctx.shape[2]
    B = 2
    L = BL // B
    BPB = NB // B
    NU = NB * G
    TT = TB // P
    SCALE = float(D) ** -0.5
    TINY = 1e-30
    RS = 3
    KR = 3 * D + 1

    def split(u):
        return u // G, u % G

    def slot_uses(u):
        t, g = split(u)
        per_block = len([h for h in range(G) if h % RS == g % RS])
        return per_block * t + g // RS + 1

    def slot_before(u):
        g = u % G
        return next(v for v in range(u - 1, u - 2 * G, -1) if v % G % RS == g % RS)

    def out_tile(s):
        t, g = split(s)
        t, k = (t - 1, g - 1) if g >= 1 else (t - 2, G - 1)
        return (t, k) if 0 <= t < NB else None

    def x_split_at(s):
        t, g = split(s)
        return t + 1 if g == 3 and 0 <= t < NB - 1 else None

    def attn_split_at(s):
        t, g = split(s)
        return t - 1 if g == 0 and 1 <= t <= NB else None

    STEPS = range(-2, NU + G + 2)

    DVE_CHUNKS, POOL_CHUNKS = (1, 3), (0, 2, 4)
    DVE_HEADS, POOL_HEADS = (0,), (1, 2, 3)

    with ExitStack() as stack:
        def sb(name, shape, dt, into=stack):
            return into.enter_context(nc.sbuf_tensor(name, shape, dt))

        def sem(name):
            return stack.enter_context(nc.semaphore(name))

        wq_hi = sb("wq_hi", [P, G, C], F32R)
        wq_lo = sb("wq_lo", [P, G, C], F32R)
        wo_hi = sb("wo_hi", [P, G, C], F32R)
        wo_lo = sb("wo_lo", [P, G, C], F32R)
        k_packed = sb("k_packed", [P, G, HG, BL], F32R)
        k_diag = sb("k_diag", [P, G, B, HG * L], F32R)
        v_hi = sb("v_hi", [L, B, C], F16)
        v_lo = sb("v_lo", [L, B, C], F16)
        v_scale = sb("v_scale", [P, G], F32)
        v_inv = sb("v_inv", [P, G], F32)
        bias = sb("bias", [P, G], F32)
        ident = sb("ident", [P, P], F32)
        ones = sb("ones", [L, D], F16)
        x_f = sb("x_f", [P, G, TB], F32)
        x_hi = sb("x_hi", [P, G, TB], F32R)
        x_lo = sb("x_lo", [P, G, TB], F32R)
        q_hi = sb("q_hi", [P, RS, TB], F32R)
        q_lo = sb("q_lo", [P, RS, TB], F32R)
        q_packed = sb("q_packed", [P, RS, HG, TB], F32R)
        mx = sb("mx", [P, RS, HG, TT], F32)
        mxT = sb("mxT", [HG * TT, RS, P], F32R)

        early = ExitStack()
        stage_a = sb("stage_a", [P, CC, C], F32, early)
        stage_b = sb("stage_b", [P, CC, C], F32, early)
        ctx_sb = sb("ctx_sb", [P, CC, BL], F32, early)
        vT = sb("vT", [P, G, BL], F32, early)
        k_hi = sb("k_hi", [P, G, BL], F32R, early)
        k_lo = sb("k_lo", [P, G, BL], F32R, early)
        early.close()
        p_f = sb("p_f", [L, 2, TB], F32)
        p_hi = sb("p_hi", [L, HG, TB], F16)
        p_lo = sb("p_lo", [L, HG, TB], F16)
        rden = sb("rden", [P, TB], F32)
        attn = sb("attn", [P, G, TB], F32)
        attn_hi = sb("attn_hi", [P, G, TB], F32R)
        attn_lo = sb("attn_lo", [P, G, TB], F32R)
        x_res = sb("x_res", [P, RS, TB], F32)
        out_sb = sb("out_sb", [P, RS, TB], F32)

        def bank(name):
            return stack.enter_context(nc.psum_tensor(name, [P, 512], F32))

        ps_q, ps_o, ps_pv, ps_den = bank("ps_q"), bank("ps_o"), bank("ps_pv"), bank("ps_den")
        ps_s = [bank("ps_s0"), bank("ps_s1")]
        ps_m = [bank("ps_m0"), bank("ps_m1")]
        ps_v = [ps_s[0], ps_s[1], ps_pv, ps_den]
        ps_mT = ps_m[0][0:HG * TT, 512 - P:512]

        wq_in, wk_in, wv_in, wo_in, ctx_in, bias_in = (sem(n) for n in (
            "wq_in", "wk_in", "wv_in", "wo_in", "ctx_in", "bias_in"))
        wq_hi_done, wq_lo_done, wo_hi_done, wo_lo_done = (sem(n) for n in (
            "wq_hi_done", "wq_lo_done", "wo_hi_done", "wo_lo_done"))
        zero_done, const_done, diag_done, kpack_in = (sem(n) for n in ("zero_done", "const_done", "diag_done", "kpack_in"))
        kproj_done, khi_done, klo_done = (sem(n) for n in ("kproj_done", "khi_done", "klo_done"))
        vproj_done, vmax_done, vinv_done, vT_done, vtr_done, vhi_done, vlo_done = (sem(n) for n in (
            "vproj_done", "vmax_done", "vinv_done", "vT_done", "vtr_done", "vhi_done", "vlo_done"))
        x_in, xhi_done, xlo_dve, xlo_pool = sem("x_in"), sem("xhi_done"), sem("xlo_dve"), sem("xlo_pool")
        q_done, qhi_done, qlo_done = sem("q_done"), sem("qhi_done"), sem("qlo_done")
        pack_in = [sem(f"pack_in{i}") for i in range(RS)]
        PACK = 16 * (2 * HG + 1)
        ms_done, max_done, mT_done, mT_copied = sem("ms_done"), sem("max_done"), sem("mT_done"), sem("mT_copied")
        s_done, pf_done, phi_done = sem("s_done"), sem("pf_done"), sem("phi_done")
        plo_dve, plo_pool = sem("plo_dve"), sem("plo_pool")
        packhi_done = sem("packhi_done")
        pv_done, rden_done, norm_done = sem("pv_done"), sem("rden_done"), sem("norm_done")
        ahi_done, alo_dve, alo_pool = sem("ahi_done"), sem("alo_dve"), sem("alo_pool")
        o_done, outs_done = sem("o_done"), sem("outs_done")
        res_in = [sem(f"res_in{i}") for i in range(RS)]
        out_in = [sem(f"out_in{i}") for i in range(RS)]

        block = stack.enter_context(nc.Block())

        @block.sync
        def _(sp):
            sp.dma_start(stage_a[:, 0:G, :], wq).then_inc(wq_in, 16)
            sp.dma_start(x_f[:, :, :], x[0]).then_inc(x_in, 16)
            sp.dma_start(ctx_sb[:, :, :], ctx).then_inc(ctx_in, 16)
            sp.dma_start(stage_b[:, :, :], wk).then_inc(wk_in, 16)
            sp.dma_start(bias[:, :], bo).then_inc(bias_in, 16)
            sp.wait_ge(wq_hi_done, G)
            sp.wait_ge(wq_lo_done, G)
            sp.dma_start(stage_a[:, :, :], wv).then_inc(wv_in, 16)
            sp.wait_ge(kproj_done, G)
            sp.dma_start(stage_b[:, 0:G, :], wo).then_inc(wo_in, 16)
            sp.wait_ge(khi_done, G)
            sp.wait_ge(klo_done, G)
            for i in range(HG):
                for row, src in ((0, k_hi), (D, k_hi), (2 * D, k_lo)):
                    sp.dma_start(k_packed[row:row + D, :, i, :].bitcast(F32),
                                 src[D * i:D * (i + 1), :, :].bitcast(F32)).then_inc(kpack_in, 16)

            def load_x(t):
                sp.wait_ge(xhi_done, G * t)
                sp.wait_ge(xlo_dve, len(DVE_CHUNKS) * t)
                sp.wait_ge(xlo_pool, len(POOL_CHUNKS) * t)
                sp.dma_start(x_f[:, :, :], x[t]).then_inc(x_in, 16)

            def load_max(u):
                t, g = split(u)
                sp.wait_ge(mT_copied, u + 1)
                if slot_before(u) >= 0:
                    sp.wait_ge(s_done, HG * (slot_before(u) + 1))
                sp.dma_start(q_packed[3 * D:KR, g % RS, :, :].bitcast(F32).rearrange("o i (a c) -> o (i a) c", c=P),
                             mxT[:, g % RS, :].bitcast(F32)).then_inc(pack_in[g % RS], 16)

            def pack_q(u):
                t, g = split(u)
                if slot_before(u) >= 0:
                    sp.wait_ge(s_done, HG * (slot_before(u) + 1))
                sp.wait_ge(qhi_done, u + 1)
                for row, src, done in ((2 * D, q_hi, None), (D, q_lo, qlo_done)):
                    if done is not None:
                        sp.wait_ge(done, u + 1)
                    for i in range(HG):
                        sp.dma_start(q_packed[row:row + D, g % RS, i, :].bitcast(F32),
                                     src[D * i:D * (i + 1), g % RS, :].bitcast(F32)).then_inc(pack_in[g % RS], 16)

            for s in STEPS:
                if 0 <= s + 1 < NU:
                    load_max(s + 1)
                if 0 <= s + 2 < NU:
                    pack_q(s + 2)
                if s % G == 3 and 0 <= s // G + 2 < NB:
                    load_x(s // G + 2)

        @block.gpsimd
        def _(pool):
            nc.gpsimd.memset(k_diag[:, :, :, :].bitcast(F32), 0.0).then_inc(const_done, 1)
            pool.wait_ge(const_done, 1)
            nc.gpsimd.memset(k_packed[3 * D:KR, :, :, :].bitcast(F32), -1.0).then_inc(const_done, 1)
            pool.wait_ge(const_done, 2)
            nc.gpsimd.memset(ones[:, :], 1.0).then_inc(const_done, 1)
            pool.wait_ge(const_done, 3)
            nc.gpsimd.memset(ident[:, :], 0.0).then_inc(zero_done, 1)
            pool.wait_ge(zero_done, 1)
            nc.gpsimd.affine_select(out=ident[:, :], in_=ident[:, :], compare_op=ALU.not_equal, fill=1.0,
                                    base=0, pattern=[[-1, P]], channel_multiplier=1).then_inc(const_done, 1)

            def x_low(t, chunks):
                for c in chunks:
                    pool.wait_ge(xhi_done, G * t + c + 1)
                    nc.gpsimd.tensor_tensor(x_lo[:, c, :], x_f[:, c, :], x_hi[:, c, :].bitcast(F32),
                                            ALU.subtract).then_inc(xlo_pool, 1)

            def p_low(u, i):
                pool.wait_ge(phi_done, HG * u + i + 1)
                pool.wait_ge(pf_done, HG * u + i + 1)
                if u >= 1:
                    pool.wait_ge(pv_done, u)
                nc.gpsimd.tensor_tensor(p_lo[:, i, :], p_f[:, i % 2, :], p_hi[:, i, :],
                                        ALU.subtract).then_inc(plo_pool, 1)

            x_low(0, POOL_CHUNKS)
            pool.wait_ge(wo_in, 16)
            for c in range(G):
                pool.wait_ge(wo_hi_done, c + 1)
                nc.gpsimd.tensor_tensor(wo_lo[:, c, :], stage_b[:, c, :], wo_hi[:, c, :].bitcast(F32),
                                        ALU.subtract).then_inc(wo_lo_done, 1)

            for s in STEPS:
                xt, at = x_split_at(s), attn_split_at(s)
                if xt is not None:
                    x_low(xt, POOL_CHUNKS[:2])
                if 0 <= s < NU:
                    p_low(s, 1)
                    p_low(s, 2)
                if xt is not None:
                    x_low(xt, POOL_CHUNKS[2:])
                if 0 <= s < NU:
                    p_low(s, 3)
                if at is not None:
                    for c in POOL_CHUNKS:
                        pool.wait_ge(ahi_done, G * at + c + 1)
                        nc.gpsimd.tensor_tensor(attn_lo[:, c, :], attn[:, c, :], attn_hi[:, c, :].bitcast(F32),
                                                ALU.subtract).then_inc(alo_pool, 1)

        @block.scalar
        def _(act):
            def x_high(t, chunks):
                act.wait_ge(x_in, 16 * (t + 1))
                if t >= 1:
                    act.wait_ge(q_done, G * t)
                for c in chunks:
                    nc.scalar.copy(x_hi[:, c, :], x_f[:, c, :]).then_inc(xhi_done, 1)

            act.wait_ge(wq_in, 16)
            for c in range(G):
                nc.scalar.copy(wq_hi[:, c, :], stage_a[:, c, :]).then_inc(wq_hi_done, 1)
            x_high(0, range(G))

            def q_high(u):
                t, g = split(u)
                act.wait_ge(q_done, u + 1)
                if slot_before(u) >= 0:
                    act.wait_ge(s_done, HG * (slot_before(u) + 1))
                nc.scalar.copy(q_hi[:, g % RS, :], ps_q[:, :]).then_inc(qhi_done, 1)
                act.wait_ge(qhi_done, u + 1)
                for i in range(HG):
                    nc.scalar.copy(q_packed[0:D, g % RS, i, :],
                                   q_hi[D * i:D * (i + 1), g % RS, :].bitcast(F32)).then_inc(packhi_done, 1)

            def start_k():
                for g in range(G):
                    act.wait_ge(kproj_done, g + 1)
                    nc.scalar.copy(k_hi[:, g, :], ps_s[g % 2][:, 0:BL]).then_inc(khi_done, 1)
                act.wait_ge(const_done, 1)
                act.wait_ge(khi_done, G)
                for i in range(HG):
                    for b in range(B):
                        rows = slice(D * i, D * (i + 1))
                        nc.scalar.copy(k_diag[rows, :, b, L * i:L * (i + 1)],
                                       k_hi[rows, :, L * b:L * (b + 1)].bitcast(F32)).then_inc(diag_done, 1)

            def start_v():
                for g in range(G):
                    act.wait_ge(vtr_done, B * (g + 1))
                    nc.scalar.copy(v_hi[:, :, P * g:P * (g + 1)],
                                   ps_v[g % 4][0:L, 0:B * P].rearrange("l (b c) -> l b c", b=B)).then_inc(vhi_done, 1)

            def split_wo():
                act.wait_ge(wo_in, 16)
                for c in range(G):
                    nc.scalar.copy(wo_hi[:, c, :], stage_b[:, c, :]).then_inc(wo_hi_done, 1)

            def attn_high(t, chunks):
                for c in chunks:
                    act.wait_ge(norm_done, G * t + c + 1)
                    if t >= 1:
                        act.wait_ge(o_done, G * t)
                    nc.scalar.copy(attn_hi[:, c, :], attn[:, c, :]).then_inc(ahi_done, 1)

            def exponentials(u, i):
                n = HG * u + i
                act.wait_ge(s_done, n + 1)
                if n >= 2:
                    before = n - 2
                    if before % HG in DVE_HEADS:
                        act.wait_ge(plo_dve, before // HG + 1)
                    else:
                        act.wait_ge(plo_pool, len(POOL_HEADS) * (before // HG) + POOL_HEADS.index(before % HG) + 1)
                nc.scalar.activation(p_f[:, i % 2, :], ps_s[i % 2][0:L, :], ACT.Exp,
                                     scale=SCALE).then_inc(pf_done, 1)
                if u >= 1:
                    act.wait_ge(pv_done, u)
                nc.scalar.activation(p_hi[:, i, :], ps_s[i % 2][0:L, :], ACT.Exp,
                                     scale=SCALE).then_inc(phi_done, 1)

            for s in STEPS:
                if s == 0:
                    act.wait_ge(wo_lo_done, G)
                    act.wait_ge(vlo_done, G)
                    act.wait_ge(kpack_in, 16 * 3 * HG)
                xt, at = x_split_at(s), attn_split_at(s)
                if 0 <= s < NU:
                    exponentials(s, 0)
                    exponentials(s, 1)
                if xt is not None:
                    x_high(xt, range(0, 3))
                if out_tile(s - 1) is not None:
                    t, k = out_tile(s - 1)
                    act.wait_ge(outs_done, G * t + k + 1)
                    act.dma_start(out[t, k], out_sb[:, k % RS, :]).then_inc(out_in[k % RS], 16)
                if 0 <= s < NU:
                    exponentials(s, 2)
                if xt is not None:
                    x_high(xt, range(3, G))
                if at is not None:
                    attn_high(at, (0, 1))
                if 0 <= s < NU:
                    exponentials(s, 3)
                if 0 <= s + 1 < NU:
                    g = (s + 1) % G
                    act.wait_ge(mT_done, s + 2)
                    if slot_before(s + 1) >= 0:
                        act.wait_ge(s_done, HG * (slot_before(s + 1) + 1))
                    nc.scalar.copy(mxT[:, g % RS, :], ps_mT).then_inc(mT_copied, 1)
                if at is not None:
                    attn_high(at, (2, 3))
                if out_tile(s + 1) is not None:
                    t, k = out_tile(s + 1)
                    n = G * t + k
                    if slot_before(n) >= 0:
                        act.wait_ge(outs_done, slot_before(n) + 1)
                    else:
                        act.wait_ge(phi_done, 1)
                    act.dma_start(x_res[:, k % RS, :], x[t, :, k, :]).then_inc(res_in[k % RS], 16)
                if 0 <= s + 2 < NU:
                    q_high(s + 2)
                if at is not None:
                    attn_high(at, (4,))
                if s == -2:
                    start_k()
                    start_v()
                    split_wo()
            for i in range(RS):
                act.wait_ge(out_in[i], 16 * NB * len([k for k in range(G) if k % RS == i]))

        @block.vector
        def _(dve):
            dve.wait_ge(wq_in, 16)
            for c in range(G):
                dve.wait_ge(wq_hi_done, c + 1)
                nc.vector.tensor_tensor(wq_lo[:, c, :], stage_a[:, c, :], wq_hi[:, c, :].bitcast(F32),
                                        ALU.subtract).then_inc(wq_lo_done, 1)

            def q_low(u):
                t, g = split(u)
                dve.wait_ge(qhi_done, u + 1)
                nc.vector.tensor_tensor(q_lo[:, g % RS, :], ps_q[:, :], q_hi[:, g % RS, :].bitcast(F32),
                                        ALU.subtract).then_inc(qlo_done, 1)

            def start_k():
                for g in range(G):
                    dve.wait_ge(khi_done, g + 1)
                    nc.vector.tensor_tensor(k_lo[:, g, :], ps_s[g % 2][:, 0:BL], k_hi[:, g, :].bitcast(F32),
                                            ALU.subtract).then_inc(klo_done, 1)

            def start_v():
                for g in range(G):
                    dve.wait_ge(vproj_done, g + 1)
                    nc.vector.tensor_reduce(v_scale[:, g:g + 1], ps_v[(g + 2) % 4][:, 0:BL], AX_X, ALU.max,
                                            apply_absolute_value=True).then_inc(vmax_done, 1)
                    dve.wait_ge(vmax_done, 3 * g + 1)
                    nc.vector.tensor_scalar(v_scale[:, g:g + 1], v_scale[:, g:g + 1], TINY, None,
                                            ALU.max).then_inc(vmax_done, 1)
                    dve.wait_ge(vmax_done, 3 * g + 2)
                    nc.vector.reciprocal(v_inv[:, g:g + 1], v_scale[:, g:g + 1]).then_inc(vmax_done, 1)
                    dve.wait_ge(vmax_done, 3 * g + 3)
                    nc.vector.tensor_scalar(vT[:, g, :], ps_v[(g + 2) % 4][:, 0:BL], v_inv[:, g:g + 1], None,
                                            ALU.mult).then_inc(vT_done, 1)
                for g in range(G):
                    dve.wait_ge(vhi_done, g + 1)
                    nc.vector.tensor_tensor(v_lo[:, :, P * g:P * (g + 1)],
                                            ps_v[g % 4][0:L, 0:B * P].rearrange("l (b c) -> l b c", b=B),
                                            v_hi[:, :, P * g:P * (g + 1)], ALU.subtract).then_inc(vlo_done, 1)
                dve.wait_ge(bias_in, 16)

            def reduce_max(u, tt):
                g = u % G
                dve.wait_ge(ms_done, TT * u + tt + 1)
                if slot_before(u) >= 0:
                    dve.wait_ge(mT_done, slot_before(u) + 1)
                nc.vector.tensor_reduce(mx[:, g % RS, :, tt],
                                        ps_m[tt % 2][:, 0:HG * L].rearrange("p (h k) -> p h k", k=L),
                                        AX_X, ALU.max).then_inc(max_done, 1)

            def invert_den(u, half):
                cols = slice(TB // 2 * half, TB // 2 * (half + 1))
                nc.vector.reciprocal(rden[:, cols], ps_den[:, cols]).then_inc(rden_done, 1)

            def normalise(u):
                t, g = split(u)
                dve.wait_ge(rden_done, 2 * (u + 1))
                if t >= 1:
                    dve.wait_ge(ahi_done, G * t)
                    dve.wait_ge(alo_dve, len(DVE_CHUNKS) * t)
                    dve.wait_ge(alo_pool, len(POOL_CHUNKS) * t)
                nc.vector.scalar_tensor_tensor(attn[:, g, :], ps_pv[:, :], v_scale[:, g:g + 1], rden[:, :],
                                               ALU.mult, ALU.mult).then_inc(norm_done, 1)

            def p_low(u, i):
                dve.wait_ge(phi_done, HG * u + i + 1)
                dve.wait_ge(pf_done, HG * u + i + 1)
                nc.vector.tensor_tensor(p_lo[:, i, :], p_f[:, i % 2, :], p_hi[:, i, :],
                                        ALU.subtract).then_inc(plo_dve, 1)

            def x_low(t):
                for c in DVE_CHUNKS:
                    dve.wait_ge(xhi_done, G * t + c + 1)
                    nc.vector.tensor_tensor(x_lo[:, c, :], x_f[:, c, :], x_hi[:, c, :].bitcast(F32),
                                            ALU.subtract).then_inc(xlo_dve, 1)

            def attn_low(t, c):
                dve.wait_ge(ahi_done, G * t + c + 1)
                nc.vector.tensor_tensor(attn_lo[:, c, :], attn[:, c, :], attn_hi[:, c, :].bitcast(F32),
                                        ALU.subtract).then_inc(alo_dve, 1)

            def finish_out(t, k):
                n = G * t + k
                dve.wait_ge(o_done, n + 1)
                dve.wait_ge(res_in[k % RS], 16 * slot_uses(n))
                if slot_before(n) >= 0:
                    dve.wait_ge(out_in[k % RS], 16 * (slot_uses(n) - 1))
                nc.vector.scalar_tensor_tensor(out_sb[:, k % RS, :], ps_o[:, :], bias[:, k:k + 1],
                                               x_res[:, k % RS, :], ALU.add, ALU.add).then_inc(outs_done, 1)

            x_low(0)
            for s in STEPS:
                xt, at = x_split_at(s), attn_split_at(s)
                if 0 <= s + 1 < NU:
                    reduce_max(s + 1, 0)
                    reduce_max(s + 1, 1)
                if 0 <= s - 1 < NU:
                    dve.wait_ge(pv_done, s)
                    invert_den(s - 1, 0)
                if 0 <= s + 1 < NU:
                    reduce_max(s + 1, 2)
                    reduce_max(s + 1, 3)
                if 0 <= s < NU:
                    p_low(s, 0)
                if xt is not None:
                    x_low(xt)
                if 0 <= s - 1 < NU:
                    invert_den(s - 1, 1)
                    normalise(s - 1)
                if out_tile(s) is not None:
                    finish_out(*out_tile(s))
                if at is not None:
                    attn_low(at, 1)
                if 0 <= s + 2 < NU:
                    q_low(s + 2)
                if at is not None:
                    attn_low(at, 3)
                if s == -2:
                    start_k()
                    start_v()

        @block.tensor
        def _(pe):
            def project(ps, w_hi, w_lo, a_hi, a_lo, k, part, ready=None):
                for c in part:
                    if ready is not None:
                        ready(c)
                    for n, (w, a) in enumerate(((w_hi, a_hi), (w_lo, a_hi), (w_hi, a_lo))):
                        last = nc.tensor.matmul(ps[:, :], w[:, c, P * k:P * (k + 1)], a[:, c, :],
                                                start=(c == 0 and n == 0), stop=(c == G - 1 and n == MM32 - 1))
                return last

            def wait_chunk(hi, lo_dve, lo_pool, t, c):
                pe.wait_ge(hi, G * t + c + 1)
                if c in DVE_CHUNKS:
                    pe.wait_ge(lo_dve, len(DVE_CHUNKS) * t + DVE_CHUNKS.index(c) + 1)
                else:
                    pe.wait_ge(lo_pool, len(POOL_CHUNKS) * t + POOL_CHUNKS.index(c) + 1)

            def project_q(u):
                t, g = split(u)

                def ready(c):
                    if u == 0:
                        pe.wait_ge(wq_hi_done, c + 1)
                        pe.wait_ge(wq_lo_done, c + 1)
                    if g == 0:
                        wait_chunk(xhi_done, xlo_dve, xlo_pool, t, c)
                if u >= 1:
                    pe.wait_ge(qlo_done, u)
                project(ps_q, wq_hi, wq_lo, x_hi, x_lo, g, range(G), ready).then_inc(q_done, 1)

            def project_ctx(w, ps, g):
                for c in range(CC):
                    last = nc.tensor.matmul(ps[:, 0:BL], w[:, c, P * g:P * (g + 1)], ctx_sb[:, c, :],
                                            start=(c == 0), stop=(c == CC - 1))
                return last

            def start_k():
                pe.wait_ge(wk_in, 16)
                pe.wait_ge(ctx_in, 16)
                for g in range(G):
                    if g >= 2:
                        pe.wait_ge(klo_done, g - 1)
                    project_ctx(stage_b, ps_s[g % 2], g).then_inc(kproj_done, 1)

            def start_v():
                pe.wait_ge(wv_in, 16)
                for g in range(G):
                    if g < 4:
                        pe.wait_ge(klo_done, min(G, 4 + g))
                    else:
                        pe.wait_ge(vT_done, g - 3)
                    project_ctx(stage_a, ps_v[(g + 2) % 4], g).then_inc(vproj_done, 1)
                pe.wait_ge(const_done, 4)
                pe.wait_ge(vT_done, G)
                for g in range(G):
                    if g >= 4:
                        pe.wait_ge(vlo_done, g - 3)
                    for b in range(B):
                        nc.tensor.transpose(ps_v[g % 4][0:L, P * b:P * (b + 1)], vT[:, g, L * b:L * (b + 1)],
                                            ident[:, :]).then_inc(vtr_done, 1)

            def max_scores(u, tt):
                t, g = split(u)
                pe.wait_ge(qhi_done, u + 1)
                if tt >= 2:
                    pe.wait_ge(max_done, TT * u + tt - 1)
                elif u >= 1:
                    pe.wait_ge(max_done, TT * (u - 1) + tt + 3)
                    pe.wait_ge(mT_copied, u)
                nc.tensor.matmul(ps_m[tt % 2][:, 0:HG * L], q_hi[:, g % RS, P * tt:P * (tt + 1)],
                                 k_diag[:, g, t // BPB, :], start=True, stop=True).then_inc(ms_done, 1)

            def transpose_max(u):
                pe.wait_ge(max_done, TT * (u + 1))
                nc.tensor.transpose(ps_mT, mx[:, u % G % RS, :, :].rearrange("p i t -> p (i t)"),
                                    ident[:, :]).then_inc(mT_done, 1)

            def scores(u, i):
                t, g = split(u)
                b = t // BPB
                if i == 0:
                    pe.wait_ge(pack_in[g % RS], PACK * slot_uses(u))
                    pe.wait_ge(packhi_done, HG * (u + 1))
                if HG * u + i >= 2:
                    pe.wait_ge(phi_done, HG * u + i - 1)
                nc.tensor.matmul(ps_s[i % 2][0:L, :], k_packed[0:KR, g, i, L * b:L * (b + 1)],
                                 q_packed[0:KR, g % RS, i, :], start=True, stop=True).then_inc(s_done, 1)

            def values(u):
                t, g = split(u)
                b = t // BPB
                pe.wait_ge(phi_done, HG * (u + 1))
                pe.wait_ge(plo_dve, len(DVE_HEADS) * (u + 1))
                pe.wait_ge(plo_pool, len(POOL_HEADS) * (u + 1))
                if u >= 1:
                    pe.wait_ge(norm_done, u)
                for n, (v, p) in enumerate(((v_hi, p_hi), (v_lo, p_hi), (v_hi, p_lo))):
                    for i in range(HG):
                        nc.tensor.matmul(ps_pv[D * i:D * (i + 1), :], v[:, b, P * g + D * i:P * g + D * (i + 1)],
                                         p[:, i, :], start=(n == 0), stop=(n == 2), tile_position=(0, D * i))
                for n, p in enumerate((p_hi, p_lo)):
                    for i in range(HG):
                        last = nc.tensor.matmul(ps_den[D * i:D * (i + 1), :], ones[:, :], p[:, i, :],
                                                start=(n == 0), stop=(n == 1), tile_position=(0, D * i))
                last.then_inc(pv_done, 1)

            def project_out(t, k, part):
                n = G * t + k

                def ready(c):
                    if k == 0:
                        wait_chunk(ahi_done, alo_dve, alo_pool, t, c)
                if part[0] == 0 and n >= 1:
                    pe.wait_ge(outs_done, n)
                last = project(ps_o, wo_hi, wo_lo, attn_hi, attn_lo, k, part, ready)
                if part[-1] == G - 1:
                    last.then_inc(o_done, 1)

            for s in STEPS:
                if s == 0:
                    pe.wait_ge(vlo_done, G)
                    pe.wait_ge(kpack_in, 16 * 3 * HG)
                if s == -1:
                    pe.wait_ge(diag_done, HG * B)
                if s == G + 1:
                    pe.wait_ge(wo_hi_done, G)
                    pe.wait_ge(wo_lo_done, G)
                max_unit = s + 1 if 0 <= s + 1 < NU else None
                tile = out_tile(s)
                if 0 <= s - 1 < NU:
                    values(s - 1)
                if max_unit is not None:
                    max_scores(max_unit, 0)
                    max_scores(max_unit, 1)
                if 0 <= s < NU:
                    scores(s, 0)
                    scores(s, 1)
                if tile is not None:
                    project_out(*tile, range(0, 3))
                if max_unit is not None:
                    max_scores(max_unit, 2)
                    max_scores(max_unit, 3)
                if 0 <= s < NU:
                    scores(s, 2)
                if tile is not None:
                    project_out(*tile, range(3, G))
                if 0 <= s < NU:
                    scores(s, 3)
                if max_unit is not None:
                    transpose_max(max_unit)
                if 0 <= s + 2 < NU:
                    project_q(s + 2)
                if s == -2:
                    start_k()
                    start_v()


def kernel(x, ctx_2048, L0_xattn_Wq, L0_xattn_Wk, L0_xattn_Wv, L0_xattn_Wk_ip, L0_xattn_Wv_ip, L0_xattn_Wo,
           L0_xattn_bo):
    import concourse.bacc as bacc
    from concourse.bass_utils import run_bass_kernel_spmd

    Bn, S, C = x.shape
    _, L, CC = ctx_2048.shape
    G = C // P
    NB = Bn * S // TB

    def w_layout(w):
        w = np.asarray(w)
        return np.ascontiguousarray(w.reshape(w.shape[0], -1, P).transpose(2, 1, 0))

    arrays = {
        "x": np.ascontiguousarray(np.asarray(x).reshape(NB, TB, G, P).transpose(0, 3, 2, 1)),
        "ctx": w_layout(np.asarray(ctx_2048).reshape(Bn * L, CC)),
        "wq": w_layout(L0_xattn_Wq),
        "wk": w_layout(L0_xattn_Wk),
        "wv": w_layout(L0_xattn_Wv),
        "wo": w_layout(L0_xattn_Wo),
        "bo": np.ascontiguousarray(np.asarray(L0_xattn_bo).reshape(G, P).T),
    }
    nc = bacc.Bacc("TRN2", target_bir_lowering=False, num_devices=1)
    aps = [nc.dram_tensor(f"in_{n}", a.shape, mybir.dt.from_np(a.dtype), kind="ExternalInput").ap()
           for n, a in arrays.items()]
    out = nc.dram_tensor("out", (NB, G, P, TB), F32, kind="ExternalOutput").ap()
    xattn_kernel(nc, *aps, out)
    r = run_bass_kernel_spmd(nc, [{f"in_{n}": a for n, a in arrays.items()}], core_ids=[0])
    got = r.results[0]["out"]
    return got.transpose(0, 3, 1, 2).reshape(Bn, S, C)
```

```python
import numpy as np
from contextlib import ExitStack

import concourse.bass as bass
from concourse import mybir

F32 = mybir.dt.float32
F32R = mybir.dt.float32r
F16 = mybir.dt.float16
ALU = mybir.AluOpType
ACT = mybir.ActivationFunctionType
AX_X = mybir.AxisListType.X

HEADS = 20
P = 128
TB = 512


def xattn_kernel(nc, x, ctx, wq, wk, wv, wo, bo, out):
    NB, _, G, _ = x.shape
    C = G * P
    HG = HEADS // G
    D = C // HEADS
    CC = ctx.shape[1]
    BL = ctx.shape[2]
    B = 2
    L = BL // B
    BPB = NB // B
    NU = NB * G
    TT = TB // P
    SCALE = float(D) ** -0.5
    TINY = 1e-30
    WARM_UP = 8
    RS = 3
    KR = 3 * D + 1

    def exists(t):
        return not isinstance(t, int) or 0 <= t < NB

    def shift(t, g, n):
        return t + (g + n) // G, (g + n) % G

    def nth(t, g):
        return t * G + g

    def slot_uses(t, g):
        return t * len(range(g % RS, G, RS)) + g // RS + 1

    def slot_before(t, g):
        back = next(n for n in range(1, 2 * G) if (g - n) % G % RS == g % RS)
        return shift(t, g, -back)

    def out_tiles(t, g):
        if isinstance(t, int):
            if (t, g) == (NB - 1, G - 2):
                return [(NB - 2, G - 3), (NB - 2, G - 2)]
            if (t, g) == (NB - 1, G - 1):
                return [(NB - 2, G - 1)]
            if t >= NB or (t, g) < (1, 1):
                return []
        return [(t - 1, g - 1) if g >= 1 else (t - 2, G - 1)]

    def filling(t, g):
        return isinstance(t, int) and t * G + g <= G

    def value_group(t, g):
        return (nth(t, g) + 1,) if isinstance(t, int) and -1 <= nth(t, g) < G - 1 else ()

    def query_group(t, g):
        return (nth(t, g) + 3,) if isinstance(t, int) and -2 <= nth(t, g) < G - 3 else ()

    def wo_chunks(t, g):
        return {0: (0, 1), G - 1: ()}.get(g, (g + 1,)) if isinstance(t, int) and t == 0 else ()

    def is_last(t):
        return isinstance(t, int) and t == NB - 1

    def x_split_at(t, g):
        if g != 3 or (isinstance(t, int) and not 1 <= t < NB - 1):
            return None
        return t + 1

    def attn_split_at(t, g):
        if isinstance(t, int) and (t, g) == (NB - 1, G - 1):
            return NB - 1, (0, 1, 2)
        if isinstance(t, int) and t == NB:
            return NB - 1, (3, 4) if g == 0 else ()
        return (t - 1, range(G)) if g == 0 and exists(t - 1) else (t, ())

    def run(engine, step, first, end):
        for g in (G - 2, G - 1):
            step(-1, g)
        for t in range(first):
            for g in range(G):
                step(t, g)
        with engine.Fori(first, end) as t:
            for g in range(G):
                step(t, g)
        for t in range(end, NB):
            for g in range(G):
                step(t, g)
        step(NB, 0)

    LOOP = (2, NB - 2)
    LOOP_PE = (BPB + 1, NB - 1)

    DVE_CHUNKS, POOL_CHUNKS = (1, 3), (0, 2, 4)
    DVE_HEADS, POOL_HEADS = (0,), (1, 2, 3)
    TOP_ACT, TOP_DVE = (0, 1, 2), (3,)

    with ExitStack() as stack:
        def sb(name, shape, dt, into=stack):
            return into.enter_context(nc.sbuf_tensor(name, shape, dt))

        def sem(name):
            return stack.enter_context(nc.semaphore(name))

        def sems(name, n):
            return [sem(f"{name}{i}") for i in range(n)]

        wq_hi = sb("wq_hi", [P, G, C], F32R)
        with ExitStack() as start_up:
            wq_sb = sb("wq_sb", [P, G, C], F32, start_up)
        wq_lo = sb("wq_lo", [P, G, C], F32R)
        wo_hi = sb("wo_hi", [P, G, C], F32R)
        with ExitStack() as start_up:
            wo_sb = sb("wo_sb", [P, G, C], F32, start_up)
        wo_lo = sb("wo_lo", [P, G, C], F32R)
        k_packed = sb("k_packed", [P, G, HG, BL], F32R)
        k_diag = sb("k_diag", [P, G, B, HG * L], F32R)
        v_hi = sb("v_hi", [L, B, C], F16)
        v_lo = sb("v_lo", [L, B, C], F16)
        v_scale = sb("v_scale", [P, G], F32)
        v_inv = sb("v_inv", [P, G], F32)
        bias = sb("bias", [P, G], F32)
        ident = sb("ident", [P, P], F32)
        ones = sb("ones", [L, D], F16)
        x_f = sb("x_f", [P, G, TB], F32)
        x_hi = sb("x_hi", [P, G, TB], F32R)
        x_lo = sb("x_lo", [P, G, TB], F32R)
        q_hi = sb("q_hi", [P, RS, TB], F32R)
        q_lo = sb("q_lo", [P, RS, TB], F32R)
        q_packed = sb("q_packed", [P, RS, HG, TB], F32R)
        mx = sb("mx", [P, RS, HG, TT], F32)
        mxT = sb("mxT", [HG * TT, RS, P], F32R)

        with ExitStack() as start_up:
            wk_sb = sb("wk_sb", [P, CC, C], F32, start_up)
            k_hi = sb("k_hi", [P, G, BL], F32R, start_up)
            k_lo = sb("k_lo", [P, G, BL], F32R, start_up)
        p_f = sb("p_f", [L, HG, TB], F32)
        p_hi = sb("p_hi", [L, HG, TB], F16)
        p_lo = sb("p_lo", [L, HG, TB], F16)
        rden = sb("rden", [P, TB], F32)
        attn = sb("attn", [P, G, TB], F32)
        with ExitStack() as start_up:
            wv_sb = sb("wv_sb", [P, G, CC * P], F32, start_up)
            ctx_sb = sb("ctx_sb", [P, CC, BL], F32, start_up)
            vT = sb("vT", [P, BL], F32, start_up)
        attn_hi = sb("attn_hi", [P, G, TB], F32R)
        attn_lo = sb("attn_lo", [P, G, TB], F32R)
        x_res = sb("x_res", [P, RS, TB], F32)
        out_sb = sb("out_sb", [P, RS, TB], F32)

        def bank(name):
            return stack.enter_context(nc.psum_tensor(name, [P, 512], F32))

        ps_q, ps_o, ps_pv, ps_den = bank("ps_q"), bank("ps_o"), bank("ps_pv"), bank("ps_den")
        ps_s = [bank("ps_s0"), bank("ps_s1")]
        ps_m = [bank("ps_m0"), bank("ps_m1")]
        ps_mT = ps_m[0][0:HG * TT, 512 - P:512]
        ps_k = [ps_s[0], ps_s[1], ps_pv, ps_den, ps_o]
        ps_v, ps_vt = ps_o[:, 0:BL], ps_o[0:L, 512 - B * P:512]
        ps_last = [ps_q, ps_m[0], ps_m[1], ps_o, ps_s[0]]

        def out_bank(t, k):
            if is_last(t):
                return ps_last[k]
            return ps_q if isinstance(t, int) and (t, k) == (NB - 2, G - 2) else ps_o

        bias_in, ctx_in = sem("bias_in"), sems("ctx_in", CC // 2)
        wq_in, wo_in, x_in = sems("wq_in", G), sems("wo_in", G), sems("x_in", G)
        wk_in, wv_in = sems("wk_in", CC), sems("wv_in", G)
        kpack_in, ktop_done, kmid_done = sem("kpack_in"), sem("ktop_done"), sem("kmid_done")
        wq_hi_done, wq_lo_done = sem("wq_hi_done"), sem("wq_lo_done")
        wo_hi_done, wo_lo_done = sem("wo_hi_done"), sem("wo_lo_done")
        warm_ready = sem("warm_ready")
        zero_done, const_done = sem("zero_done"), sem("const_done")
        kproj_done, khi_done, klo_done, diag_done = sem("kproj_done"), sem("khi_done"), sem("klo_done"), sem("diag_done")
        vproj_done, vscale_done, vT_done = sem("vproj_done"), sem("vscale_done"), sem("vT_done")
        vtr_done, vhi_done, vlo_done = sem("vtr_done"), sem("vhi_done"), sem("vlo_done")
        xhi_done, xlo_dve, xlo_pool = sem("xhi_done"), sem("xlo_dve"), sem("xlo_pool")
        q_chunks, qhi_done, qlo_done = sem("q_chunks"), sem("qhi_done"), sem("qlo_done")
        qtop_act, qtop_dve = sem("qtop_act"), sem("qtop_dve")
        pack_in = sems("pack_in", RS)
        PACK = 16 * (2 * HG + 1)
        ms_done, max_done, mT_done, mT_copied = sem("ms_done"), sem("max_done"), sem("mT_done"), sem("mT_copied")
        s_done, pf_done, phi_done = sem("s_done"), sem("pf_done"), sem("phi_done")
        plo_dve, plo_pool = sem("plo_dve"), sem("plo_pool")
        pv_done, rden_done, norm_done = sem("pv_done"), sem("rden_done"), sem("norm_done")
        ahi_done, alo_dve, alo_pool = sem("ahi_done"), sem("alo_dve"), sem("alo_pool")
        o_chunks, outs_done = sem("o_chunks"), sem("outs_done")
        res_in, out_in = sems("res_in", RS), sems("out_in", RS)
        last_done, last_in = sem("last_done"), sem("last_in")

        block = stack.enter_context(nc.Block())

        @block.sync
        def _(sp):
            def load_x(t, chunks):
                for c in chunks:
                    if exists(t - 1):
                        sp.wait_ge(q_chunks, G * nth(t - 1, 0) + c + 1)
                    sp.dma_start(x_f[:, c, :], x[t, :, c, :]).then_inc(x_in[c], 16)

            for c in range(CC):
                if c % 2 == 0:
                    sp.dma_start(ctx_sb[:, c:c + 2, :], ctx[:, c:c + 2, :]).then_inc(ctx_in[c // 2], 16)
                sp.dma_start(wk_sb[:, c, :], wk[:, c, :]).then_inc(wk_in[c], 16)
            for g in range(G):
                sp.dma_start(wq_sb[:, g, :], wq[:, g, :]).then_inc(wq_in[g], 16)
                if g == 0:
                    load_x(0, range(G))
                    sp.dma_start(bias[:, :], bo).then_inc(bias_in, 16)
                sp.dma_start(wv_sb[:, g, :], wv[:, g, :]).then_inc(wv_in[g], 16)
            sp.wait_ge(klo_done, G)
            for i in range(HG):
                sp.dma_start(k_packed[2 * D:3 * D, :, i, :].bitcast(F32),
                             k_lo[D * i:D * (i + 1), :, :].bitcast(F32)).then_inc(kpack_in, 16)

            def load_max(t, g):
                sp.wait_ge(mT_copied, nth(t, g) + 1)
                sp.dma_start(q_packed[3 * D:KR, g % RS, :, :].bitcast(F32).rearrange("o i (a c) -> o (i a) c", c=P),
                             mxT[:, g % RS, :].bitcast(F32)).then_inc(pack_in[g % RS], 16)

            def pack_q(t, g):
                for row, src, done in ((2 * D, q_hi, qhi_done), (D, q_lo, qlo_done)):
                    sp.wait_ge(done, nth(t, g) + 1)
                    for i in range(HG):
                        sp.dma_start(q_packed[row:row + D, g % RS, i, :].bitcast(F32),
                                     src[D * i:D * (i + 1), g % RS, :].bitcast(F32)).then_inc(pack_in[g % RS], 16)

            def step(t, g):
                if exists(shift(t, g, 1)[0]):
                    load_max(*shift(t, g, 1))
                xt = t + 2 if g == G - 1 else t + 1
                if exists(xt) and not (isinstance(xt, int) and xt == 0):
                    early = isinstance(xt, int) and xt == 1
                    load_x(xt, ({G - 1: (0, 1), 0: (2, 3), 1: (4,)} if early else
                                {G - 1: (0,), 0: (1,), 1: (2,), 2: (3, 4)}).get(g, ()))
                for c in wo_chunks(t, g):
                    sp.dma_start(wo_sb[:, c, :], wo[:, c, :]).then_inc(wo_in[c], 16)
                if exists(shift(t, g, 2)[0]):
                    pack_q(*shift(t, g, 2))
            run(sp, step, *LOOP)

        @block.gpsimd
        def _(pool):
            nc.gpsimd.memset(k_diag[:, :, :, :].bitcast(F32), 0.0).then_inc(const_done, 1)
            pool.wait_ge(const_done, 1)
            nc.gpsimd.memset(k_packed[3 * D:KR, :, :, :].bitcast(F32), -1.0).then_inc(const_done, 1)
            pool.wait_ge(const_done, 2)
            nc.gpsimd.memset(ones[:, :], 1.0).then_inc(const_done, 1)
            pool.wait_ge(const_done, 3)
            nc.gpsimd.memset(ident[:, :], 0.0).then_inc(zero_done, 1)
            pool.wait_ge(zero_done, 1)
            nc.gpsimd.affine_select(out=ident[:, :], in_=ident[:, :], compare_op=ALU.not_equal, fill=1.0,
                                    base=0, pattern=[[-1, P]], channel_multiplier=1).then_inc(const_done, 1)

            def x_low(t, chunks):
                for c in chunks:
                    pool.wait_ge(xhi_done, G * t + c + 1)
                    nc.gpsimd.tensor_tensor(x_lo[:, c, :], x_f[:, c, :], x_hi[:, c, :].bitcast(F32),
                                            ALU.subtract).then_inc(xlo_pool, 1)

            def p_low(t, g, i):
                pool.wait_ge(phi_done, HG * nth(t, g) + i + 1)
                pool.wait_ge(pf_done, HG * nth(t, g) + i + 1)
                if exists(shift(t, g, -1)[0]):
                    pool.wait_ge(pv_done, nth(t, g))
                nc.gpsimd.tensor_tensor(p_lo[:, i, :], p_f[:, i, :], p_hi[:, i, :],
                                        ALU.subtract).then_inc(plo_pool, 1)

            def attn_low(t, chunks):
                for c in chunks:
                    pool.wait_ge(ahi_done, G * t + c + 1)
                    nc.gpsimd.tensor_tensor(attn_lo[:, c, :], attn[:, c, :], attn_hi[:, c, :].bitcast(F32),
                                            ALU.subtract).then_inc(alo_pool, 1)

            x_low(0, POOL_CHUNKS)
            for i in range(HG):
                pool.wait_ge(khi_done, G)
                if i >= 1:
                    pool.wait_ge(ktop_done, i)
                nc.gpsimd.tensor_copy(k_packed[0:D, :, i, :],
                                      k_hi[D * i:D * (i + 1), :, :].bitcast(F32)).then_inc(ktop_done, 1)

            def wo_low(c):
                pool.wait_ge(wo_hi_done, c + 1)
                nc.gpsimd.tensor_tensor(wo_lo[:, c, :], wo_sb[:, c, :], wo_hi[:, c, :].bitcast(F32),
                                        ALU.subtract).then_inc(wo_lo_done, 1)

            def step(t, g):
                xt, (at, chunks) = x_split_at(t, g), attn_split_at(t, g)
                mine = [c for c in POOL_CHUNKS if c in chunks]
                if xt is not None:
                    x_low(xt, POOL_CHUNKS[:2])
                if exists(t):
                    p_low(t, g, 1)
                if xt is not None:
                    x_low(xt, POOL_CHUNKS[2:])
                attn_low(at, mine[:1])
                if exists(t):
                    p_low(t, g, 2)
                    p_low(t, g, 3)
                attn_low(at, mine[1:])
                if isinstance(t, int) and (t, g) == (0, 2):
                    x_low(1, POOL_CHUNKS)
                for c in wo_chunks(*shift(t, g, -1)):
                    wo_low(c)

            run(pool, step, *LOOP)

        @block.scalar
        def _(act):
            def x_high(t, chunks):
                for c in chunks:
                    act.wait_ge(x_in[c], 16 * (t + 1))
                    if exists(t - 1):
                        act.wait_ge(q_chunks, G * nth(t - 1, G - 1) + c + 1)
                    nc.scalar.copy(x_hi[:, c, :], x_f[:, c, :]).then_inc(xhi_done, 1)

            def start_k():
                for g in range(G):
                    act.wait_ge(kproj_done, g + 1)
                    nc.scalar.copy(k_hi[:, g, :], ps_k[g][:, 0:BL]).then_inc(khi_done, 1)

            def diagonal_k(b, heads):
                act.wait_ge(const_done, 1)
                act.wait_ge(khi_done, G)
                for i in heads:
                    rows = slice(D * i, D * (i + 1))
                    nc.scalar.copy(k_diag[rows, :, b, L * i:L * (i + 1)],
                                   k_hi[rows, :, L * b:L * (b + 1)].bitcast(F32)).then_inc(diag_done, 1)

            def w_high(w_in, w_sb, w_hi, done, chunks):
                for c in chunks:
                    act.wait_ge(w_in[c], 16)
                    nc.scalar.copy(w_hi[:, c, :], w_sb[:, c, :]).then_inc(done, 1)

            def v_high(g):
                act.wait_ge(vtr_done, B * (g + 1))
                nc.scalar.copy(v_hi[:, :, P * g:P * (g + 1)],
                               ps_vt.rearrange("l (b c) -> l b c", b=B)).then_inc(vhi_done, 1)

            def q_high(t, g):
                act.wait_ge(q_chunks, G * (nth(t, g) + 1))
                if exists(slot_before(t, g)[0]):
                    act.wait_ge(s_done, HG * (nth(*slot_before(t, g)) + 1))
                nc.scalar.copy(q_hi[:, g % RS, :], ps_q[:, :]).then_inc(qhi_done, 1)

            def q_top(t, g):
                act.wait_ge(qhi_done, nth(t, g) + 1)
                for i in TOP_ACT:
                    nc.scalar.copy(q_packed[0:D, g % RS, i, :],
                                   q_hi[D * i:D * (i + 1), g % RS, :].bitcast(F32)).then_inc(qtop_act, 1)

            def attn_high(t, chunks):
                for c in chunks:
                    act.wait_ge(norm_done, G * t + c + 1)
                    if exists(t - 1):
                        act.wait_ge(o_chunks, G * nth(t - 1, G - 1) + c + 1)
                    nc.scalar.copy(attn_hi[:, c, :], attn[:, c, :]).then_inc(ahi_done, 1)

            def exponentials(t, g, i):
                act.wait_ge(s_done, HG * nth(t, g) + i + 1)
                if exists(shift(t, g, -1)[0]):
                    if i in DVE_HEADS:
                        act.wait_ge(plo_dve, len(DVE_HEADS) * (nth(t, g) - 1) + DVE_HEADS.index(i) + 1)
                    else:
                        act.wait_ge(plo_pool, len(POOL_HEADS) * (nth(t, g) - 1) + POOL_HEADS.index(i) + 1)
                nc.scalar.activation(p_f[:, i, :], ps_s[i % 2][0:L, :], ACT.Exp,
                                     scale=SCALE).then_inc(pf_done, 1)
                if exists(shift(t, g, -1)[0]):
                    act.wait_ge(pv_done, nth(t, g))
                nc.scalar.activation(p_hi[:, i, :], ps_s[i % 2][0:L, :], ACT.Exp,
                                     scale=SCALE).then_inc(phi_done, 1)

            def copy_max(t, g):
                act.wait_ge(mT_done, nth(t, g) + 1)
                if exists(slot_before(t, g)[0]):
                    act.wait_ge(s_done, HG * (nth(*slot_before(t, g)) + 1))
                nc.scalar.copy(mxT[:, g % RS, :], ps_mT).then_inc(mT_copied, 1)

            def load_residual(t, k):
                if is_last(t):
                    return
                if exists(slot_before(t, k)[0]):
                    act.wait_ge(outs_done, nth(*slot_before(t, k)) + 1)
                act.dma_start(x_res[:, k % RS, :], x[t, :, k, :]).then_inc(res_in[k % RS], 16)

            def store(t, k):
                act.wait_ge(outs_done, nth(t, k) + 1)
                if is_last(t):
                    act.dma_start(out[t, k], x_f[:, k, :]).then_inc(last_in, 16)
                    return
                act.dma_start(out[t, k], out_sb[:, k % RS, :]).then_inc(out_in[k % RS], 16)

            w_high(wq_in, wq_sb, wq_hi, wq_hi_done, (0,))
            x_high(0, range(G))
            start_k()
            diagonal_k(0, range(HG))

            def step(t, g):
                xt, (at, chunks) = x_split_at(t, g), attn_split_at(t, g)
                if xt is not None:
                    x_high(xt, range(0, 3))
                if exists(t):
                    exponentials(t, g, 0)
                    exponentials(t, g, 1)
                for tile in out_tiles(*shift(t, g, -1)):
                    store(*tile)
                if xt is not None:
                    x_high(xt, range(3, G))
                attn_high(at, [c for c in (0, 1) if c in chunks])
                if exists(t):
                    exponentials(t, g, 2)
                for v in value_group(t, g):
                    v_high(v)
                if exists(shift(t, g, 1)[0]):
                    copy_max(*shift(t, g, 1))
                if exists(t):
                    exponentials(t, g, 3)
                attn_high(at, [c for c in (2, 3) if c in chunks])
                if exists(shift(t, g, 1)[0]):
                    q_top(*shift(t, g, 1))
                for tile in out_tiles(*shift(t, g, 1)):
                    load_residual(*tile)
                attn_high(at, [c for c in (4,) if c in chunks])
                if exists(shift(t, g, 2)[0]):
                    q_high(*shift(t, g, 2))
                if isinstance(t, int) and (t, g) == (0, 2):
                    x_high(1, range(G))
                w_high(wq_in, wq_sb, wq_hi, wq_hi_done, query_group(t, g))
                if isinstance(t, int) and (t, g) == (-1, G - 2):
                    for i in range(HG):
                        nc.scalar.copy(k_packed[D:2 * D, :, i, :],
                                       k_hi[D * i:D * (i + 1), :, :].bitcast(F32)).then_inc(kmid_done, 1)
                if isinstance(t, int) and t == 0 and g <= 1:
                    diagonal_k(1, range(HG // 2 * g, HG // 2 * (g + 1)))
                w_high(wo_in, wo_sb, wo_hi, wo_hi_done, wo_chunks(*shift(t, g, -1)))

            run(act, step, *LOOP)
            for k in range(G):
                store(NB - 1, k)
            for i in range(RS):
                act.wait_ge(out_in[i], 16 * (NB - 1) * len(range(i, G, RS)))
            act.wait_ge(last_in, 16 * G)

        @block.vector
        def _(dve):
            def start_k():
                for g in range(G):
                    dve.wait_ge(khi_done, g + 1)
                    nc.vector.tensor_tensor(k_lo[:, g, :], ps_k[g][:, 0:BL], k_hi[:, g, :].bitcast(F32),
                                            ALU.subtract).then_inc(klo_done, 1)

            def wq_low(chunks):
                for c in chunks:
                    dve.wait_ge(wq_hi_done, c + 1)
                    nc.vector.tensor_tensor(wq_lo[:, c, :], wq_sb[:, c, :],
                                            wq_hi[:, c, :].bitcast(F32), ALU.subtract).then_inc(wq_lo_done, 1)

            def scale_v(g):
                dve.wait_ge(vproj_done, g + 1)
                nc.vector.tensor_reduce(v_scale[:, g:g + 1], ps_v, AX_X, ALU.max,
                                        apply_absolute_value=True).then_inc(vscale_done, 1)
                dve.wait_ge(vscale_done, 3 * g + 1)
                nc.vector.tensor_scalar(v_scale[:, g:g + 1], v_scale[:, g:g + 1], TINY, None,
                                        ALU.max).then_inc(vscale_done, 1)
                dve.wait_ge(vscale_done, 3 * g + 2)
                nc.vector.reciprocal(v_inv[:, g:g + 1], v_scale[:, g:g + 1]).then_inc(vscale_done, 1)
                dve.wait_ge(vscale_done, 3 * g + 3)
                nc.vector.tensor_scalar(vT[:, :], ps_v, v_inv[:, g:g + 1], None, ALU.mult).then_inc(vT_done, 1)

            def v_low(g):
                dve.wait_ge(vhi_done, g + 1)
                nc.vector.tensor_tensor(v_lo[:, :, P * g:P * (g + 1)], ps_vt.rearrange("l (b c) -> l b c", b=B),
                                        v_hi[:, :, P * g:P * (g + 1)], ALU.subtract).then_inc(vlo_done, 1)

            def x_low(t, chunks):
                for c in chunks:
                    dve.wait_ge(xhi_done, G * t + c + 1)
                    nc.vector.tensor_tensor(x_lo[:, c, :], x_f[:, c, :], x_hi[:, c, :].bitcast(F32),
                                            ALU.subtract).then_inc(xlo_dve, 1)

            def q_low(t, g):
                dve.wait_ge(qhi_done, nth(t, g) + 1)
                nc.vector.tensor_tensor(q_lo[:, g % RS, :], ps_q[:, :], q_hi[:, g % RS, :].bitcast(F32),
                                        ALU.subtract).then_inc(qlo_done, 1)

            def q_top(t, g):
                dve.wait_ge(qhi_done, nth(t, g) + 1)
                for i in TOP_DVE:
                    nc.vector.tensor_copy(q_packed[0:D, g % RS, i, :],
                                          q_hi[D * i:D * (i + 1), g % RS, :].bitcast(F32)).then_inc(qtop_dve, 1)

            def reduce_max(t, g, tt):
                dve.wait_ge(ms_done, TT * nth(t, g) + tt + 1)
                if exists(slot_before(t, g)[0]):
                    dve.wait_ge(mT_done, nth(*slot_before(t, g)) + 1)
                nc.vector.tensor_reduce(mx[:, g % RS, :, tt],
                                        ps_m[tt % 2][:, 0:HG * L].rearrange("p (h k) -> p h k", k=L),
                                        AX_X, ALU.max).then_inc(max_done, 1)

            def p_low(t, g, i):
                dve.wait_ge(phi_done, HG * nth(t, g) + i + 1)
                dve.wait_ge(pf_done, HG * nth(t, g) + i + 1)
                nc.vector.tensor_tensor(p_lo[:, i, :], p_f[:, i, :], p_hi[:, i, :],
                                        ALU.subtract).then_inc(plo_dve, 1)

            def invert_den(t, g, half):
                cols = slice(TB // 2 * half, TB // 2 * (half + 1))
                dve.wait_ge(pv_done, nth(t, g) + 1)
                nc.vector.reciprocal(rden[:, cols], ps_den[:, cols]).then_inc(rden_done, 1)

            def normalise(t, g):
                dve.wait_ge(rden_done, 2 * (nth(t, g) + 1))
                if exists(t - 1):
                    if g in DVE_CHUNKS:
                        dve.wait_ge(alo_dve, len(DVE_CHUNKS) * (t - 1) + DVE_CHUNKS.index(g) + 1)
                    else:
                        dve.wait_ge(alo_pool, len(POOL_CHUNKS) * (t - 1) + POOL_CHUNKS.index(g) + 1)
                nc.vector.scalar_tensor_tensor(attn[:, g, :], ps_pv[:, :], v_scale[:, g:g + 1], rden[:, :],
                                               ALU.mult, ALU.mult).then_inc(norm_done, 1)

            def attn_low(t, c):
                dve.wait_ge(ahi_done, G * t + c + 1)
                nc.vector.tensor_tensor(attn_lo[:, c, :], attn[:, c, :], attn_hi[:, c, :].bitcast(F32),
                                        ALU.subtract).then_inc(alo_dve, 1)

            def finish_out(t, k):
                if is_last(t):
                    dve.wait_ge(last_done, k + 1)
                    nc.vector.scalar_tensor_tensor(x_f[:, k, :], out_bank(t, k)[:, :], bias[:, k:k + 1],
                                                   x_f[:, k, :], ALU.add, ALU.add).then_inc(outs_done, 1)
                    return
                dve.wait_ge(o_chunks, G * (nth(t, k) + 1))
                dve.wait_ge(res_in[k % RS], 16 * slot_uses(t, k))
                if exists(slot_before(t, k)[0]):
                    dve.wait_ge(out_in[k % RS], 16 * slot_uses(*slot_before(t, k)))
                nc.vector.scalar_tensor_tensor(out_sb[:, k % RS, :], out_bank(t, k)[:, :], bias[:, k:k + 1],
                                               x_res[:, k % RS, :], ALU.add, ALU.add).then_inc(outs_done, 1)

            nc.vector.memset(v_hi[:, 0, 0:TB], 1.0).then_inc(warm_ready, 1)
            wq_low((0,))
            x_low(0, DVE_CHUNKS)
            start_k()
            dve.wait_ge(bias_in, 16)

            def step(t, g):
                xt, (at, chunks) = x_split_at(t, g), attn_split_at(t, g)
                last_t, last_g = shift(t, g, -1)
                if isinstance(t, int) and t == NB:
                    attn_low(at, 3)
                if xt is not None:
                    x_low(xt, DVE_CHUNKS[:1])
                for v in value_group(t, g):
                    scale_v(v)
                if exists(shift(t, g, 1)[0]):
                    reduce_max(*shift(t, g, 1), 0)
                    reduce_max(*shift(t, g, 1), 1)
                if exists(t):
                    p_low(t, g, 0)
                if exists(shift(t, g, 1)[0]):
                    reduce_max(*shift(t, g, 1), 2)
                    reduce_max(*shift(t, g, 1), 3)
                if xt is not None:
                    x_low(xt, DVE_CHUNKS[1:])
                if exists(last_t):
                    invert_den(last_t, last_g, 0)
                for v in value_group(t, g):
                    v_low(v)
                if exists(last_t):
                    invert_den(last_t, last_g, 1)
                    normalise(last_t, last_g)
                if exists(shift(t, g, 1)[0]):
                    q_top(*shift(t, g, 1))
                for tile in out_tiles(t, g):
                    finish_out(*tile)
                if 1 in chunks:
                    attn_low(at, 1)
                if exists(shift(t, g, 2)[0]):
                    q_low(*shift(t, g, 2))
                if 1 in chunks and 3 in chunks:
                    attn_low(at, 3)
                wq_low(query_group(t, g))
                if isinstance(t, int) and (t, g) == (0, 2):
                    x_low(1, DVE_CHUNKS)

            run(dve, step, *LOOP)
            for k in range(G):
                finish_out(NB - 1, k)

        @block.tensor
        def _(pe):
            def warm_up():
                pe.wait_ge(warm_ready, 1)
                for _ in range(WARM_UP):
                    nc.tensor.matmul(ps_q[:, :], v_hi[:, 0, 0:P], v_hi[:, 0, 0:TB], start=True, stop=True)

            def start_k():
                for c in range(CC):
                    pe.wait_ge(ctx_in[c // 2], 16)
                    pe.wait_ge(wk_in[c], 16)
                    for g in range(G):
                        last = nc.tensor.matmul(ps_k[g][:, 0:BL], wk_sb[:, c, P * g:P * (g + 1)], ctx_sb[:, c, :],
                                                start=(c == 0), stop=(c == CC - 1))
                        if c == CC - 1:
                            last.then_inc(kproj_done, 1)

            def project_v(g):
                if g == 0:
                    pe.wait_ge(klo_done, G)
                else:
                    pe.wait_ge(vlo_done, g)
                pe.wait_ge(wv_in[g], 16)
                for c in range(CC):
                    last = nc.tensor.matmul(ps_v, wv_sb[:, g, P * c:P * (c + 1)], ctx_sb[:, c, :],
                                            start=(c == 0), stop=(c == CC - 1))
                last.then_inc(vproj_done, 1)

            def transpose_v(g):
                pe.wait_ge(const_done, 4)
                pe.wait_ge(vT_done, g + 1)
                for b in range(B):
                    nc.tensor.transpose(ps_vt[:, P * b:P * (b + 1)], vT[:, L * b:L * (b + 1)],
                                        ident[:, :]).then_inc(vtr_done, 1)

            def project(ps, w_hi, w_lo, a_hi, a_lo, k, chunks, ready, done):
                for c in chunks:
                    ready(c)
                    for n, (w, a) in enumerate(((w_hi, a_hi), (w_lo, a_hi), (w_hi, a_lo))):
                        last = nc.tensor.matmul(ps[:, :], w[:, k, P * c:P * (c + 1)], a[:, c, :],
                                                start=(c == 0 and n == 0), stop=(c == G - 1 and n == 2))
                    last.then_inc(done, 1)

            def wait_chunk(hi, lo_dve, lo_pool, t, c):
                pe.wait_ge(hi, G * t + c + 1)
                if c in DVE_CHUNKS:
                    pe.wait_ge(lo_dve, len(DVE_CHUNKS) * t + DVE_CHUNKS.index(c) + 1)
                else:
                    pe.wait_ge(lo_pool, len(POOL_CHUNKS) * t + POOL_CHUNKS.index(c) + 1)

            def project_q(t, g, chunks):
                def ready(c):
                    if isinstance(t, int) and t == 0 and c == 0:
                        pe.wait_ge(wq_hi_done, g + 1)
                        pe.wait_ge(wq_lo_done, g + 1)
                    if g == 0:
                        wait_chunk(xhi_done, xlo_dve, xlo_pool, t, c)
                if 0 in chunks and exists(shift(t, g, -1)[0]):
                    pe.wait_ge(qlo_done, nth(t, g))
                project(ps_q, wq_hi, wq_lo, x_hi, x_lo, g, chunks, ready, q_chunks)

            def max_scores(t, g, tt, b):
                if tt == 0:
                    pe.wait_ge(qhi_done, nth(t, g) + 1)
                if tt >= 2:
                    pe.wait_ge(max_done, TT * nth(t, g) + tt - 1)
                elif exists(shift(t, g, -1)[0]):
                    pe.wait_ge(max_done, TT * (nth(t, g) - 1) + tt + 3)
                    pe.wait_ge(mT_copied, nth(t, g))
                nc.tensor.matmul(ps_m[tt % 2][:, 0:HG * L], q_hi[:, g % RS, P * tt:P * (tt + 1)],
                                 k_diag[:, g, b, :], start=True, stop=True).then_inc(ms_done, 1)

            def transpose_max(t, g):
                pe.wait_ge(max_done, TT * (nth(t, g) + 1))
                nc.tensor.transpose(ps_mT, mx[:, g % RS, :, :].rearrange("p i t -> p (i t)"),
                                    ident[:, :]).then_inc(mT_done, 1)

            def scores(t, g, i, b):
                if i == 0:
                    pe.wait_ge(pack_in[g % RS], PACK * slot_uses(t, g))
                    pe.wait_ge(qtop_act, len(TOP_ACT) * (nth(t, g) + 1))
                    pe.wait_ge(qtop_dve, len(TOP_DVE) * (nth(t, g) + 1))
                if i >= 2 or exists(shift(t, g, -1)[0]):
                    pe.wait_ge(phi_done, HG * nth(t, g) + i - 1)
                nc.tensor.matmul(ps_s[i % 2][0:L, :], k_packed[0:KR, g, i, L * b:L * (b + 1)],
                                 q_packed[0:KR, g % RS, i, :], start=True, stop=True).then_inc(s_done, 1)

            def values(t, g, b):
                def attend(v, p, **flags):
                    for i in range(HG):
                        nc.tensor.matmul(ps_pv[D * i:D * (i + 1), :], v[:, b, P * g + D * i:P * g + D * (i + 1)],
                                         p[:, i, :], tile_position=(0, D * i), **flags)

                def add_up(p, **flags):
                    for i in range(HG):
                        last = nc.tensor.matmul(ps_den[D * i:D * (i + 1), :], ones[:, :], p[:, i, :],
                                                tile_position=(0, D * i), **flags)
                    return last

                pe.wait_ge(phi_done, HG * (nth(t, g) + 1))
                if exists(shift(t, g, -1)[0]):
                    pe.wait_ge(norm_done, nth(t, g))
                attend(v_hi, p_hi, start=True, stop=False)
                attend(v_lo, p_hi, start=False, stop=False)
                add_up(p_hi, start=True, stop=False)
                pe.wait_ge(plo_dve, len(DVE_HEADS) * (nth(t, g) + 1))
                pe.wait_ge(plo_pool, len(POOL_HEADS) * (nth(t, g) + 1))
                attend(v_hi, p_lo, start=False, stop=True)
                add_up(p_lo, start=False, stop=True).then_inc(pv_done, 1)

            def project_out(t, k, chunks):
                def ready(c):
                    if k == 0:
                        wait_chunk(ahi_done, alo_dve, alo_pool, t, c)
                if chunks[0] == 0 and out_bank(t, k) is ps_q:
                    pe.wait_ge(qlo_done, NU)
                elif chunks[0] == 0 and exists(shift(t, k, -1)[0]):
                    pe.wait_ge(outs_done, nth(t, k))
                project(out_bank(t, k), wo_hi, wo_lo, attn_hi, attn_lo, k, chunks, ready, o_chunks)

            def last_tiles(c):
                wait_chunk(ahi_done, alo_dve, alo_pool, NB - 1, c)
                for k in range(G):
                    if c == 0 and k == 0:
                        pe.wait_ge(outs_done, nth(NB - 2, G - 1))
                    if c == 0 and k == 1:
                        pe.wait_ge(max_done, TT * NU)
                        pe.wait_ge(mT_copied, NU)
                    if c == 0 and k == 3:
                        pe.wait_ge(outs_done, nth(NB - 1, 0))
                    if c == 0 and k == 4:
                        pe.wait_ge(phi_done, HG * NU)
                    for n, (w, a) in enumerate(((wo_hi, attn_hi), (wo_lo, attn_hi), (wo_hi, attn_lo))):
                        last = nc.tensor.matmul(ps_last[k][:, :], w[:, k, P * c:P * (c + 1)], a[:, c, :],
                                                start=(c == 0 and n == 0), stop=(c == G - 1 and n == 2))
                    if c == G - 1:
                        last.then_inc(last_done, 1)

            warm_up()
            start_k()

            def batch(t):
                return t // BPB if isinstance(t, int) else B - 1

            def fill(t, g):
                max_t, max_g = shift(t, g, 1)
                last_t, last_g = shift(t, g, -1)
                query = shift(t, g, 2)
                if (t, g) == (-1, G - 2):
                    project_q(*query, range(G))
                    return
                if (t, g) == (-1, G - 1):
                    pe.wait_ge(diag_done, HG)
                    pe.wait_ge(klo_done, G)
                for v in value_group(t, g):
                    project_v(v)
                if value_group(t, g):
                    max_scores(max_t, max_g, 0, batch(max_t))
                    max_scores(max_t, max_g, 1, batch(max_t))
                if (t, g) == (0, 0):
                    pe.wait_ge(kpack_in, 16 * HG)
                    pe.wait_ge(kmid_done, HG)
                    pe.wait_ge(ktop_done, HG)
                if exists(t):
                    scores(t, g, 0, batch(t))
                    scores(t, g, 1, batch(t))
                if exists(last_t):
                    pe.wait_ge(vlo_done, nth(t, g))
                    values(last_t, last_g, batch(last_t))
                if not value_group(t, g):
                    max_scores(max_t, max_g, 0, batch(max_t))
                    max_scores(max_t, max_g, 1, batch(max_t))
                project_q(*query, (0,))
                max_scores(max_t, max_g, 2, batch(max_t))
                max_scores(max_t, max_g, 3, batch(max_t))
                if exists(t):
                    scores(t, g, 2, batch(t))
                for v in value_group(t, g):
                    transpose_v(v)
                if exists(t):
                    scores(t, g, 3, batch(t))
                before = 2 if value_group(t, g) else 1
                project_q(*query, range(1, before))
                transpose_max(max_t, max_g)
                project_q(*query, range(before, G))

            def step(t, g):
                max_t, max_g = shift(t, g, 1)
                last_t, last_g = shift(t, g, -1)
                tiles = out_tiles(t, g)
                if filling(t, g):
                    fill(t, g)
                    return
                if isinstance(t, int) and (t, g) == (1, 1):
                    pe.wait_ge(wo_hi_done, G)
                    pe.wait_ge(wo_lo_done, G)
                    pe.wait_ge(diag_done, HG * B)
                values(last_t, last_g, batch(last_t))
                if exists(t):
                    scores(t, g, 0, batch(t))
                    scores(t, g, 1, batch(t))
                if exists(max_t):
                    max_scores(max_t, max_g, 0, batch(max_t))
                    max_scores(max_t, max_g, 1, batch(max_t))
                if tiles:
                    project_out(*tiles[0], (0, 1))
                if exists(max_t):
                    max_scores(max_t, max_g, 2, batch(max_t))
                    max_scores(max_t, max_g, 3, batch(max_t))
                if exists(t):
                    scores(t, g, 2, batch(t))
                if tiles:
                    project_out(*tiles[0], (2, 3))
                if exists(t):
                    scores(t, g, 3, batch(t))
                if exists(max_t):
                    transpose_max(max_t, max_g)
                if tiles:
                    project_out(*tiles[0], (4,))
                if exists(shift(t, g, 2)[0]):
                    project_q(*shift(t, g, 2), range(G))
                for tile in tiles[1:]:
                    project_out(*tile, range(G))
                if isinstance(t, int) and (t, g) == (NB - 1, G - 1):
                    last_tiles(0)
                if isinstance(t, int) and t == NB:
                    for c in range(1, G):
                        last_tiles(c)

            run(pe, step, *LOOP_PE)


def kernel(x, ctx_2048, L0_xattn_Wq, L0_xattn_Wk, L0_xattn_Wv, L0_xattn_Wk_ip, L0_xattn_Wv_ip, L0_xattn_Wo,
           L0_xattn_bo):
    import concourse.bacc as bacc
    from concourse.bass_utils import run_bass_kernel_spmd

    Bn, S, C = x.shape
    _, L, CC = ctx_2048.shape
    G = C // P
    NB = Bn * S // TB

    def w_layout(w):
        w = np.asarray(w)
        return np.ascontiguousarray(w.reshape(w.shape[0], -1, P).transpose(2, 1, 0))

    def by_group(w):
        w = w_layout(w)
        return np.ascontiguousarray(w.reshape(P, -1, G, P).transpose(0, 2, 1, 3).reshape(P, G, -1))

    arrays = {
        "x": np.ascontiguousarray(np.asarray(x).reshape(NB, TB, G, P).transpose(0, 3, 2, 1)),
        "ctx": w_layout(np.asarray(ctx_2048).reshape(Bn * L, CC)),
        "wq": by_group(L0_xattn_Wq),
        "wk": w_layout(L0_xattn_Wk),
        "wv": by_group(L0_xattn_Wv),
        "wo": by_group(L0_xattn_Wo),
        "bo": np.ascontiguousarray(np.asarray(L0_xattn_bo).reshape(G, P).T),
    }
    nc = bacc.Bacc("TRN2", target_bir_lowering=False, num_devices=1)
    aps = [nc.dram_tensor(f"in_{n}", a.shape, mybir.dt.from_np(a.dtype), kind="ExternalInput").ap()
           for n, a in arrays.items()]
    out = nc.dram_tensor("out", (NB, G, P, TB), F32, kind="ExternalOutput").ap()
    xattn_kernel(nc, *aps, out)
    r = run_bass_kernel_spmd(nc, [{f"in_{n}": a for n, a in arrays.items()}], core_ids=[0])
    got = r.results[0]["out"]
    return got.transpose(0, 3, 1, 2).reshape(Bn, S, C)
```
